# Optimizing a Trainium2 kernel written in Bass

```python
import numpy as np
import jax
import jax.numpy as jnp

def _softmax(x, axis=-1):
    return jax.nn.softmax(x, axis=axis)

def _gelu(x):
    return jax.nn.gelu(x, approximate=True)

def _silu(x):
    return jax.nn.silu(x)

def _sigmoid(x):
    return jax.nn.sigmoid(x)

def _layernorm(x, axis=-1, eps=1e-05):
    m = jnp.mean(x, axis=axis, keepdims=True)
    v = jnp.var(x, axis=axis, keepdims=True)
    return (x - m) / jnp.sqrt(v + eps)

def _scatter_add(tgt, idx, src, axis=0):
    return tgt.at[idx].add(src)

def _segment_sum(src, seg, n):
    return jax.ops.segment_sum(src, seg, n)
kernel_name = 'mk_adj_resnorm_d1_adj_r2_f9843b'

def setup_inputs(seed: int=0):
    np.random.seed(seed)
    _w = jnp.asarray

    def _rec_inputs():
        import jax
        import jax.numpy as jnp
        _gk = jax.random.key(seed)
        x = -0.0002928 + 1 * jax.random.normal(jax.random.fold_in(_gk, 1), (8192, 256), jnp.float32)
        _a = jax.random.bernoulli(jax.random.fold_in(_gk, 2), 0.000976562, (8192, 8192))
        _a = jnp.logical_or(_a, jnp.swapaxes(_a, -1, -2))
        _a = jnp.logical_or(_a, jnp.eye(8192, dtype=bool))
        adj = _a.astype(jnp.int32)
        return (x, adj)
    x, adj = _rec_inputs()

    def _L0_gnn_setup():
        import jax, jax.numpy as jnp
        import numpy as np
        N = 4096
        IN_F = 256
        OUT_F = 256
        ALPHA = 0.2
        NEG_INF = -9000000000000000.0
        key = jax.random.key(seed)
        k1, k2, k3, k4, k5 = jax.random.split(key, 5)
        x = jax.random.normal(k1, (N, IN_F), dtype=jnp.float32)
        adj = jax.random.randint(k2, (N, N), 0, 2, dtype=jnp.int32)
        W = jax.random.normal(k3, (OUT_F, IN_F), dtype=jnp.float32) / np.sqrt(IN_F)
        a1 = jax.random.normal(k4, (OUT_F,), dtype=jnp.float32) / np.sqrt(2 * OUT_F)
        a2 = jax.random.normal(k5, (OUT_F,), dtype=jnp.float32) / np.sqrt(2 * OUT_F)
        return {'x': x, 'adj': adj, 'W': W, 'a1': a1, 'a2': a2}
    _L0_gnn_all = _L0_gnn_setup()
    _L0_gnn_in = {k: v for k, v in _L0_gnn_all.items() if k in ('W', 'a1', 'a2')}
    del _L0_gnn_all
    return {'x': x, 'adj': adj, 'L0_gnn_W': _L0_gnn_in['W'], 'L0_gnn_a1': _L0_gnn_in['a1'], 'L0_gnn_a2': _L0_gnn_in['a2']}

def reference(x, adj, L0_gnn_W, L0_gnn_a1, L0_gnn_a2):
    import jax
    import jax.numpy as jnp

    def _L0_gnn_ref(x, adj, W, a1, a2):
        import jax, jax.numpy as jnp
        import numpy as np
        N = 4096
        IN_F = 256
        OUT_F = 256
        ALPHA = 0.2
        NEG_INF = -9000000000000000.0
        h = x @ W.T
        src = h @ a1
        dst = h @ a2
        e = jax.nn.leaky_relu(src[:, None] + dst[None, :], negative_slope=ALPHA)
        e = jnp.where(adj == 0, jnp.float32(NEG_INF), e)
        attention = jax.nn.softmax(e, axis=1)
        h_prime = attention @ h
        return h_prime
    x = _layernorm(x + _L0_gnn_ref(x, adj, L0_gnn_W, L0_gnn_a1, L0_gnn_a2), axis=-1)
    return x

_drawn_inputs = setup_inputs


def setup_inputs(seed=0):
    import zlib

    import numpy as np

    out = dict(_drawn_inputs(seed))
    spreads = {}
    factors = {}
    for name, (base, spread) in spreads.items():
        noise = np.random.default_rng([zlib.crc32(name.encode()), seed]).standard_normal(out[name].shape)
        drawn = base * np.exp(spread * noise) if base else spread * noise
        out[name] = jnp.asarray(drawn.astype(out[name].dtype))
    for name, factor in factors.items():
        out[name] = (out[name] * factor).astype(out[name].dtype)
    return out
```

```python
from contextlib import ExitStack

import concourse.bass as bass
from concourse import mybir

F32 = mybir.dt.float32
F32R = mybir.dt.float32r
BF16 = mybir.dt.bfloat16
I32 = mybir.dt.int32
ALU = mybir.AluOpType
ACT = mybir.ActivationFunctionType
AX = mybir.AxisListType

P = 128
N = 8192
F = 256
SLOPE = 0.2
EPS = 1e-5
SAFE = 30.0
LOWEST = -3.0e38
HIGHEST_EXPONENT = 60.0

TILES = 4
ROWS = TILES * P
CHUNKS = N // ROWS
BLOCKS = N // P
PAIRS = BLOCKS // 2
RING = 4
BODY = 8
BODIES = PAIRS // BODY
SLOTS = 4
COLS = N // (BODIES * SLOTS)
TOTAL = CHUNKS * BODIES
FA = F + 2
LEAD = 4
POOL_LO = (1,3,5,7)
VEC_LO = tuple(k for k in range(BODY) if k not in POOL_LO)
CREDIT = RING
LO_CREDIT = BODY
assert BODY - 1 in POOL_LO


def gat_kernel(nc, x, adj, W, a1, a2, out):
    rows_dram = nc.dram_tensor("rows_scratch", (2, N), F32, kind="Internal").ap()
    dst_dram = nc.dram_tensor("dst_scratch", (N,), F32, kind="Internal").ap()

    adj_v = adj.rearrange("(c t p) (q n) -> c q p t n", c=CHUNKS, t=TILES, p=P, n=COLS)
    x_v = x.rearrange("(c t p) f -> c p t f", c=CHUNKS, t=TILES, p=P)
    out_v = out.rearrange("(c t p) f -> c p t f", c=CHUNKS, t=TILES, p=P)
    PIECE = 1024
    PIECES = N // PIECE
    adj_rows_v = adj.rearrange("(t p) (q n) -> t q p n", p=P, n=PIECE)

    with ExitStack() as ctx:
        def sb(name, shape, dt):
            return ctx.enter_context(nc.sbuf_tensor(name, shape, dt))

        def sem(name):
            return ctx.enter_context(nc.semaphore(name))

        h_hi = sb("h_hi", [P, BLOCKS, FA], F32R)
        h_lo = sb("h_lo", [P, BLOCKS, F], F32R)
        adj_sb = sb("adj_sb", [P, SLOTS, TILES, COLS], BF16)
        w_hi = sb("w_hi", [P, RING, 2 * ROWS], F32R)
        w_lo = sb("w_lo", [P, RING, 2 * ROWS], F32R)
        weights = sb("weights", [P, RING, 2 * ROWS], F32)
        rows = sb("rows", [P, 2, ROWS], F32)
        xres = sb("xres", [P, TILES, F], F32)
        acc_sb = sb("acc_sb", [P, TILES, FA], F32)
        hsum = sb("hsum", [P, F], F32)
        ident_bf = sb("ident_bf", [P, P], BF16)
        src_dst = sb("src_dst", [P, 2, BLOCKS], F32)
        d_b = sb("d_b", [P, 2, BLOCKS], F32)
        top = sb("top", [P, 4], F32)
        top_all = sb("top_all", [P, 4], F32)
        shift = sb("shift", [P, 4], F32)
        unsafe = sb("unsafe", [P, 1], I32)
        row_stat = sb("row_stat", [P, 4, TILES], F32)
        bn = sb("bn", [P, TILES, 6], F32)
        mean_var = sb("mean_var", [P, TILES, 2], F32)

        w_t = acc_sb[:, 0:2, :]
        w_in = acc_sb[:, 2:4, 0:F]
        ident_f = xres[:, 0, 0:P]
        ab_t = xres[:, 1, 0:P]
        ab = xres[:, 2, 0:P]
        a12 = xres[:, 3, 0:4].rearrange("p (o a) -> p o a", o=2)
        ones = w_hi[:, 0, 0:P]

        t_ps = ctx.enter_context(nc.psum_tensor("t_ps", [P, RING, 512], F32))
        acc = ctx.enter_context(nc.psum_tensor("acc", [P, TILES, 512], F32))
        mask_t = t_ps[:, :, :].bitcast(BF16)

        wa_loaded = sem("wa_loaded")
        ident_step = sem("ident_step")
        ident_ready = sem("ident_ready")
        w_turned = sem("w_turned")
        wt_ready = sem("wt_ready")
        x_loaded = [sem(f"x_loaded{i}") for i in range(2)]
        x_turned = sem("x_turned")
        xt_ready = sem("xt_ready")
        h_ready = sem("h_ready")
        h_hi_ready = sem("h_hi_ready")
        h_lo_ready = sem("h_lo_ready")
        sd_ready = sem("sd_ready")
        ones_ready = sem("ones_ready")
        setup_step = sem("setup_step")
        general_step = sem("general_step")
        piece_step = sem("piece_step")
        exponent_step = sem("exponent_step")
        norm_step = sem("norm_step")
        norm_end_step = sem("norm_end_step")
        waited = sem("waited")
        top_ready = sem("top_ready")
        top_all_ready = sem("top_all_ready")
        flag_ready = sem("flag_ready")
        ab_ready = sem("ab_ready")
        db_ready = sem("db_ready")
        ab_turned = sem("ab_turned")
        abt_ready = sem("abt_ready")
        rows_written = sem("rows_written")
        hsum_done = sem("hsum_done")
        hsum_ready = sem("hsum_ready")
        dst_written = sem("dst_written")
        piece_loaded = sem("piece_loaded")
        piece_used = sem("piece_used")
        exponent_ready = sem("exponent_ready")
        adj_loaded = [sem(f"adj_loaded{i}") for i in range(SLOTS)]
        rows_loaded = sem("rows_loaded")
        mask_ready = sem("mask_ready")
        bare_ready = sem("bare_ready")
        weights_ready = sem("weights_ready")
        hi_ready = sem("hi_ready")
        lo_vec = sem("lo_vec")
        lo_pool = sem("lo_pool")
        pair_done = sem("pair_done")
        acc_done = sem("acc_done")
        acc_free = sem("acc_free")
        acc_used = sem("acc_used")
        xres_loaded = sem("xres_loaded")
        var_ready = sem("var_ready")
        std_ready = sem("std_ready")
        out_ready = sem("out_ready")
        out_written = sem("out_written")

        def low_part_count(k):
            made, s = (POOL_LO, lo_pool) if k % BODY in POOL_LO else (VEC_LO, lo_vec)
            return s, len(made), made.index(k % BODY) + 1 + len(made) * (k // BODY)

        def wait_low_part(eng, turn, k):
            s, per_turn, rank = low_part_count(k)
            eng.wait_ge(s, turn * per_turn + (LO_CREDIT + rank))

        def chain(eng, step, start):
            made = [0]

            def link(instruction):
                made[0] += 1
                instruction.then_inc(step, 1)
                eng.wait_ge(step, start + made[0])
            return link

        block = ctx.enter_context(nc.Block())

        @block.sync
        def _(sp):
            sp.dma_start(w_in, W.rearrange("(o p) k -> p o k", p=P)).then_inc(wa_loaded, 16)
            with nc.allow_non_contiguous_dma(reason="256 words each"):
                sp.dma_start(a12[:, :, 0], a1.rearrange("(o p) -> p o", p=P)).then_inc(wa_loaded, 16)
                sp.dma_start(a12[:, :, 1], a2.rearrange("(o p) -> p o", p=P)).then_inc(wa_loaded, 16)
            for g in range(2):
                sp.dma_start(weights[:, g, :].rearrange("p (t f) -> p t f", t=TILES),
                             x_v[g]).then_inc(x_loaded[g], 16)
            with sp.Fori(0, CHUNKS // 2 - 1) as u:
                for g in range(2):
                    sp.wait_ge(x_turned, u * 2 + (g + 1))
                    sp.dma_start(weights[:, g, :].rearrange("p (t f) -> p t f", t=TILES),
                                 x_v[u * 2 + (g + 2)]).then_inc(x_loaded[g], 16)
            sp.wait_ge(abt_ready, 1)
            sp.dma_start(rows_dram.rearrange("a (t p) -> (a t) p", p=P), ab_t).then_inc(rows_written, 16)
            sp.wait_ge(rows_written, 16)

            def load_rows(chunk):
                for a in range(2):
                    src = rows_dram[a:a + 1, bass.ds(chunk * ROWS, ROWS)]
                    sp.dma_start(rows[:, a, :], src.to_broadcast([P, ROWS])).then_inc(rows_loaded, 16)

            load_rows(0)
            sp.dma_start(xres[:, :, :], x_v[0]).then_inc(xres_loaded, 16)

            def serve(c, more):
                sp.wait_ge(bare_ready, c * PAIRS + PAIRS)
                load_rows(c + 1 if more else 0)
                sp.wait_ge(out_ready, c + 1)
                sp.dma_start(out_v[c], xres[:, :, :]).then_inc(out_written, 16)
                sp.wait_ge(out_written, c * 16 + 16)
                if more:
                    sp.dma_start(xres[:, :, :], x_v[c + 1]).then_inc(xres_loaded, 16)

            with sp.Fori(0, CHUNKS - 1) as c:
                serve(c, True)
            serve(CHUNKS - 1, False)

        @block.gpsimd
        def _(pool):
            nc.gpsimd.memset(ident_bf[:, :], 0.0).then_inc(ident_step, 1)
            nc.gpsimd.memset(ident_f, 0.0).then_inc(ident_step, 1)
            pool.wait_ge(ident_step, 2)
            for m in (ident_bf[:, :], ident_f):
                nc.gpsimd.affine_select(out=m, in_=m, compare_op=ALU.not_equal, fill=1.0, base=0,
                                        pattern=[[-1, P]], channel_multiplier=1).then_inc(ident_ready, 1)
            for s in range(SLOTS):
                pool.dma_start(adj_sb[:, s, :, :], adj_v[0, s]).then_inc(adj_loaded[s], 16)
            pool.wait_ge(top_ready, 1)
            nc.gpsimd.partition_all_reduce(top_all[:, :], top[:, :], P,
                                           bass.bass_isa.ReduceOp.max).then_inc(top_all_ready, 1)
            pool.sem_inc(lo_pool, LO_CREDIT)

            def turn(t, refill):
                for k in range(BODY):
                    if k in POOL_LO:
                        pool.wait_ge(hi_ready, t * BODY + (CREDIT + k + 1))
                        pool.wait_ge(pair_done, t * BODY + (CREDIT + k + 1 - RING))
                        nc.gpsimd.tensor_tensor(w_lo[:, k % RING, :], weights[:, k % RING, :],
                                                w_hi[:, k % RING, :].bitcast(F32),
                                                ALU.subtract).then_inc(lo_pool, 1)
                    if refill and k % 2 == 1:
                        nxt = t + 1
                        pool.wait_ge(mask_ready, t * BODY + (k + 1))
                        pool.dma_start(adj_sb[:, k // 2, :, :],
                                       adj_v[nxt // BODIES, (nxt % BODIES) * SLOTS + k // 2]
                                       ).then_inc(adj_loaded[k // 2], 16)

            with pool.Fori(0, TOTAL - 1) as t:
                turn(t, True)
            turn(TOTAL - 1, False)
            pool.wait_ge(mask_ready, TOTAL * BODY)
            for s in range(LEAD // 2):
                pool.dma_start(adj_sb[:, s, 0, 0:P], adj_v[0, s][:, 0, 0:P]).then_inc(adj_loaded[s], 16)

        def act_setup(act):
            with act.Fori(0, CHUNKS // 2) as u:
                for g in range(2):
                    act.wait_ge(x_turned, u * 2 + (g + 1))
                    for half in range(2):
                        last = nc.scalar.activation(weights[:, 2 + g, half * 512:(half + 1) * 512],
                                                    t_ps[:, 2 * g + half, :], ACT.Copy)
                    last.then_inc(xt_ready, 1)
                for g in range(2):
                    for t in range(TILES):
                        block_of = u * (2 * TILES) + (g * TILES + t)
                        act.wait_ge(h_ready, block_of + 1)
                        nc.scalar.activation(h_hi[:, block_of, 0:F], acc[:, t, 0:F],
                                             ACT.Copy).then_inc(h_hi_ready, 1)

        def act_main(act, general):
            act.wait_ge(ab_turned, 1)
            nc.scalar.activation(ab_t, t_ps[:, 0, 0:P], ACT.Copy).then_inc(abt_ready, 1)
            act.sem_inc(hi_ready, CREDIT)

            def exponential(s, count):
                act.wait_ge(exponent_ready, count)
                nc.scalar.activation(weights[:, s, :], weights[:, s, :], ACT.Exp).then_inc(bare_ready, 1)

            def high_part(t, k):
                act.wait_ge(weights_ready, t * BODY + (CREDIT + k + 1))
                act.wait_ge(pair_done, t * BODY + (CREDIT + k + 1 - RING))
                nc.scalar.activation(w_hi[:, k % RING, :], weights[:, k % RING, :],
                                     ACT.Copy).then_inc(hi_ready, 1)
                if general:
                    exponential((k + 1) % RING, t * BODY + (k + 2))

            def evict(c):
                act.wait_ge(acc_used, c + 1)
                for t in range(TILES):
                    if t < TILES - 1:
                        act.wait_ge(acc_done, c * (TILES - 1) + (t + 1))
                    else:
                        act.wait_ge(pair_done, c * PAIRS + (PAIRS + CREDIT))
                    nc.scalar.activation(acc_sb[:, t, :], acc[:, t, 0:FA], ACT.Copy).then_inc(acc_free, 1)

            def deviation(c):
                act.wait_ge(var_ready, c + 1)
                nc.scalar.activation(row_stat[:, 3, :], row_stat[:, 2, :], ACT.Sqrt).then_inc(std_ready, 1)

            def first_turn(c, epilogue):
                for k in range(BODY):
                    high_part(c * BODIES, k)
                    if epilogue and k == 2:
                        evict(c - 1)
                    if epilogue and k == 5:
                        deviation(c - 1)

            def other_turns(c):
                with act.Fori(1, BODIES) as b:
                    for k in range(BODY):
                        high_part(c * BODIES + b, k)

            if general:
                exponential(0, 1)
            first_turn(0, False)
            other_turns(0)
            with act.Fori(1, CHUNKS) as c:
                first_turn(c, True)
                other_turns(c)
            evict(CHUNKS - 1)
            deviation(CHUNKS - 1)

        @block.scalar
        def _(act):
            act.sem_inc(acc_free, TILES)
            act_setup(act)
            act.wait_ge(flag_ready, 1)
            flag = act.value_load(unsafe[0:1, 0:1], min_val=0, max_val=1)
            with act.If(flag < 1):
                nc.scalar.activation(d_b[:, 1, :], src_dst[:, 1, :], ACT.Exp, bias=shift[:, 0:1], scale=1.0)
                nc.scalar.activation(d_b[:, 0, :], src_dst[:, 1, :], ACT.Exp, bias=shift[:, 1:2],
                                     scale=SLOPE).then_inc(db_ready, 1)
                nc.scalar.activation(ab[:, 0:BLOCKS], src_dst[:, 0, :], ACT.Exp, bias=shift[:, 2:3],
                                     scale=SLOPE - 1.0).then_inc(ab_ready, 1)
                act_main(act, False)
            with act.Else():
                with nc.allow_non_contiguous_dma(reason="a table of 8192 words, once"):
                    act.dma_start(dst_dram.rearrange("(t p) -> p t", p=P),
                                  src_dst[:, 1, :]).then_inc(dst_written, 16)
                act.wait_ge(dst_written, 16)
                with act.Fori(0, BLOCKS) as t:
                    with act.Fori(0, PIECES) as q:
                        act.wait_ge(piece_used, t * PIECES + (q + 1))
                        act.dma_start(weights[:, 0, :].bitcast(I32), adj_rows_v[t, q]).then_inc(piece_loaded, 16)
                        act.dma_start(weights[:, 1, :],
                                      dst_dram.rearrange("(a n) -> a n", a=1)[:, bass.ds(q * PIECE, PIECE)]
                                      .to_broadcast([P, PIECE])).then_inc(piece_loaded, 16)
                act_main(act, True)

        def vec_main(dve, general):
            dve.sem_inc(weights_ready, CREDIT)
            dve.sem_inc(lo_vec, LO_CREDIT)
            dve.sem_inc(acc_used, 1)

            def bare(c, t, k, col):
                s = k % RING
                dve.wait_ge(hi_ready, t * BODY + (CREDIT + k + 1 - RING))
                wait_low_part(dve, t, k - RING)
                dve.wait_ge(rows_loaded, c * 32 + 32)
                link = chain(dve, exponent_step, (t * BODY + k) * 4)
                for j in range(2):
                    w = weights[:, s, j * ROWS:(j + 1) * ROWS]
                    if not general:
                        last = nc.vector.tensor_scalar(w, rows[:, 0, :], d_b[:, 0, bass.ds(col + j, 1)],
                                                       d_b[:, 1, bass.ds(col + j, 1)], ALU.mult, ALU.max)
                        continue
                    link(nc.vector.tensor_scalar(w, rows[:, 1, :], d_b[:, 0, bass.ds(col + j, 1)], None, ALU.add))
                    link(nc.vector.scalar_tensor_tensor(w, rows[:, 0, :], src_dst[:, 1, bass.ds(col + j, 1)], w,
                                                        ALU.add, ALU.max))
                    last = nc.vector.tensor_scalar(w, w, HIGHEST_EXPONENT, None, ALU.min)
                last.then_inc(exponent_ready if general else bare_ready, 1)

            def masked(t, k):
                dve.wait_ge(bare_ready, t * BODY + (k + 1))
                dve.wait_ge(mask_ready, t * BODY + (k + 1))
                nc.vector.scalar_tensor_tensor(weights[:, k % RING, :], mask_t[:, k % RING, :], 0.0,
                                               weights[:, k % RING, :], ALU.not_equal,
                                               ALU.mult).then_inc(weights_ready, 1)

            def low_part(t, k):
                dve.wait_ge(hi_ready, t * BODY + (CREDIT + k + 1))
                dve.wait_ge(pair_done, t * BODY + (CREDIT + k + 1 - RING))
                nc.vector.tensor_tensor(w_lo[:, k % RING, :], weights[:, k % RING, :],
                                        w_hi[:, k % RING, :].bitcast(F32), ALU.subtract).then_inc(lo_vec, 1)

            def step(c, t, b, k):
                masked(t, k)
                if k >= 1 and (k - 1) in VEC_LO:
                    low_part(t, k - 1)
                if k + 1 < BODY:
                    bare(c, t, k + 1, b * (2 * BODY) + 2 * (k + 1))

            def start_next(c, t, b):
                bare(c, t + 1, 0, (b + 1) * (2 * BODY))

            def norm_sums(c):
                dve.wait_ge(acc_free, c * TILES + 2 * TILES)
                dve.wait_ge(xres_loaded, c * 16 + 16)
                link = chain(dve, norm_step, c * 6)
                den = acc_sb[:, :, F]
                link(nc.vector.tensor_scalar(row_stat[:, 0, :], den, 0.0, None, ALU.is_equal))
                link(nc.vector.scalar_tensor_tensor(row_stat[:, 1, :], row_stat[:, 0, :], float(N), den,
                                                    ALU.mult, ALU.add))
                link(nc.vector.reciprocal(row_stat[:, 1, :], row_stat[:, 1, :]))
                for t in range(TILES):
                    last = nc.vector.scalar_tensor_tensor(acc_sb[:, t, 0:F], hsum[:, :], row_stat[:, 0, t:t + 1],
                                                          acc_sb[:, t, 0:F], ALU.mult, ALU.add)
                link(last)
                for t in range(TILES):
                    last = nc.vector.scalar_tensor_tensor(xres[:, t, :], acc_sb[:, t, 0:F], row_stat[:, 1, t:t + 1],
                                                          xres[:, t, :], ALU.mult, ALU.add)
                last.then_inc(acc_used, 1)
                dve.wait_ge(acc_used, c + 2)
                for t in range(TILES):
                    last = nc.vector.bn_stats(bn[:, t, :], xres[:, t, :])
                link(last)
                dve.sem_inc(waited, 1)
                for t in range(TILES):
                    last = nc.vector.bn_aggr(mean_var[:, t, :], bn[:, t, :])
                link(last)
                nc.vector.tensor_scalar(row_stat[:, 2, :], mean_var[:, :, 1], EPS, None,
                                        ALU.add).then_inc(var_ready, 1)

            def normalise(c):
                dve.wait_ge(std_ready, c + 1)
                link = chain(dve, norm_end_step, c)
                link(nc.vector.reciprocal(row_stat[:, 3, :], row_stat[:, 3, :]))
                for t in range(TILES):
                    last = nc.vector.tensor_scalar(xres[:, t, :], xres[:, t, :], mean_var[:, t, 0:1],
                                                   row_stat[:, 3, t:t + 1], ALU.subtract, ALU.mult)
                last.then_inc(out_ready, 1)

            def first_turn(c, epilogue):
                for k in range(BODY):
                    step(c, c * BODIES, 0, k)
                    if epilogue and k == 4:
                        norm_sums(c - 1)
                    if epilogue and k == 6:
                        normalise(c - 1)
                start_next(c, c * BODIES, 0)

            def other_turns(c):
                with dve.Fori(1, BODIES - 1) as b:
                    for k in range(BODY):
                        step(c, c * BODIES + b, b, k)
                    start_next(c, c * BODIES + b, b)
                b = BODIES - 1
                for k in range(BODY):
                    step(c, c * BODIES + b, b, k)
                bare(c + 1, c * BODIES + BODIES, 0, 0)

            bare(0, 0, 0, 0)
            first_turn(0, False)
            other_turns(0)
            with dve.Fori(1, CHUNKS) as c:
                first_turn(c, True)
                other_turns(c)
            norm_sums(CHUNKS - 1)
            normalise(CHUNKS - 1)

        @block.vector
        def _(dve):
            link = chain(dve, setup_step, 0)
            dve.sem_inc(h_lo_ready, TILES)
            dve.wait_ge(w_turned, 1)
            nc.vector.tensor_copy(w_t[:, :, 0:F], t_ps[:, 0, :].rearrange("p (k o) -> p k o", k=2))
            nc.vector.tensor_copy(w_t[:, :, F:FA],
                                  t_ps[:, 1, 0:4].rearrange("p (k a) -> p k a", k=2)).then_inc(wt_ready, 1)
            nc.vector.memset(h_hi[:, :, F:F + 1].bitcast(F32), 1.0)
            nc.vector.memset(h_hi[:, :, F + 1:FA].bitcast(F32), 0.0)
            nc.vector.memset(ones.bitcast(F32), 1.0).then_inc(ones_ready, 1)
            with dve.Fori(0, CHUNKS) as g:
                for t in range(TILES):
                    col = g * TILES + t
                    dve.wait_ge(h_hi_ready, g * TILES + (t + 1))
                    nc.vector.tensor_copy(src_dst[:, :, bass.ds(col, 1)],
                                          acc[:, t, F:FA].rearrange("p (a o) -> p a o", o=1)).then_inc(sd_ready, 1)
                    nc.vector.tensor_tensor(h_lo[:, col, :], acc[:, t, 0:F], h_hi[:, col, 0:F].bitcast(F32),
                                            ALU.subtract).then_inc(h_lo_ready, 1)
            dve.wait_ge(sd_ready, BLOCKS)
            link(nc.vector.tensor_scalar(d_b[:, :, :], src_dst[:, :, :], -1.0, None, ALU.mult))
            nc.vector.reduce_max(top[:, 0:2], src_dst[:, :, :], AX.X)
            nc.vector.reduce_max(top[:, 2:4], d_b[:, :, :], AX.X).then_inc(top_ready, 1)
            dve.wait_ge(top_all_ready, 1)
            for n, factor in enumerate((-1.0, -SLOPE, SLOPE - 1.0)):
                nc.vector.tensor_scalar(shift[:, n:n + 1], top_all[:, 1:2], factor, None, ALU.mult)
            link(nc.vector.reduce_max(shift[:, 3:4], top_all[:, :], AX.X))
            nc.vector.tensor_scalar(unsafe[:, :], shift[:, 3:4], SAFE, None, ALU.is_gt).then_inc(flag_ready, 1)
            dve.wait_ge(hsum_done, 1)
            nc.vector.tensor_copy(hsum[:, :], acc[:, 0, 0:F]).then_inc(hsum_ready, 1)
            dve.wait_ge(flag_ready, 1)
            flag = dve.value_load(unsafe[0:1, 0:1], min_val=0, max_val=1)
            with dve.If(flag < 1):
                nc.vector.memset(ab[:, BLOCKS:2 * BLOCKS], 0.0).then_inc(ab_ready, 1)
                dve.wait_ge(db_ready, 1)
                vec_main(dve, False)
            with dve.Else():
                link = chain(dve, general_step, 0)
                link(nc.vector.memset(ab[:, BLOCKS:2 * BLOCKS], LOWEST))
                dve.sem_inc(piece_used, 1)
                with dve.Fori(0, BLOCKS) as t:
                    with dve.Fori(0, PIECES) as q:
                        link = chain(dve, piece_step, (t * PIECES + q) * 3)
                        link(nc.vector.memset(weights[:, 2, :], LOWEST))
                        dve.wait_ge(piece_loaded, (t * PIECES + q) * 32 + 32)
                        dve.sem_inc(waited, 1)
                        link(nc.vector.copy_predicated(weights[:, 2, :], weights[:, 0, :].bitcast(I32),
                                                       weights[:, 1, :]))
                        link(nc.vector.reduce_max(shift[:, 0:1], weights[:, 2, :], AX.X))
                        nc.vector.tensor_tensor(ab[:, bass.ds(t + BLOCKS, 1)], ab[:, bass.ds(t + BLOCKS, 1)],
                                                shift[:, 0:1], ALU.max).then_inc(piece_used, 1)
                dve.wait_ge(piece_used, BLOCKS * PIECES + 1)
                link = chain(dve, general_step, 1)
                m, a, s = ab[:, BLOCKS:2 * BLOCKS], ab[:, 0:BLOCKS], src_dst[:, 0, :]
                link(nc.vector.tensor_tensor(m, m, s, ALU.add))
                link(nc.vector.scalar_tensor_tensor(m, m, SLOPE, m, ALU.mult, ALU.max))
                link(nc.vector.tensor_tensor(a, s, m, ALU.subtract))
                link(nc.vector.scalar_tensor_tensor(m, s, SLOPE, m, ALU.mult, ALU.subtract))
                link(nc.vector.tensor_scalar(d_b[:, 0, :], src_dst[:, 1, :], SLOPE, None, ALU.mult))
                dve.sem_inc(ab_ready, 2)
                vec_main(dve, True)

        @block.tensor
        def _(pe):
            pe.sem_inc(pair_done, CREDIT)
            pe.wait_ge(ident_ready, 2)
            pe.wait_ge(wa_loaded, 48)
            for k in range(2):
                for o in range(2):
                    nc.tensor.transpose(t_ps[:, 0, k * F + o * P:k * F + (o + 1) * P],
                                        w_in[:, o, k * P:(k + 1) * P], ident_f)
            for k in range(2):
                for o in range(2):
                    last = nc.tensor.matmul(t_ps[:, 1, 2 * k:2 * k + 2], w_in[:, o, k * P:(k + 1) * P],
                                            a12[:, o, :], start=(o == 0), stop=(o == 1))
            last.then_inc(w_turned, 1)
            pe.wait_ge(wt_ready, 1)

            with pe.Fori(0, CHUNKS // 2) as u:
                for g in range(2):
                    pe.wait_ge(x_loaded[g], u * 16 + 16)
                    for t in range(TILES):
                        for k in range(2):
                            n = (t % 2) * 2 + k
                            last = nc.tensor.transpose(t_ps[:, 2 * g + t // 2, n * P:(n + 1) * P],
                                                       weights[:, g, t * F + k * P:t * F + (k + 1) * P], ident_f)
                    last.then_inc(x_turned, 1)
                for g in range(2):
                    pe.wait_ge(xt_ready, u * 2 + (g + 1))
                    for t in range(TILES):
                        pe.wait_ge(h_lo_ready, u * (2 * TILES) + (g * TILES + t + 1))
                        for k in range(2):
                            n = t * 2 + k
                            last = nc.tensor.matmul(acc[:, t, 0:FA], weights[:, 2 + g, n * P:(n + 1) * P],
                                                    w_t[:, k, :], start=(k == 0), stop=(k == 1))
                        last.then_inc(h_ready, 1)
            pe.wait_ge(h_lo_ready, BLOCKS + TILES)
            pe.wait_ge(ones_ready, 1)
            for n in range(0, BLOCKS):
                for part in (h_hi, h_lo):
                    last = nc.tensor.matmul(acc[:, 0, 0:F], ones, part[:, n, 0:F],
                                            start=(n == 0 and part is h_hi), stop=(n == BLOCKS - 1 and part is h_lo))
            last.then_inc(hsum_done, 1)
            pe.wait_ge(ab_ready, 2)
            nc.tensor.transpose(t_ps[:, 0, 0:P], ab, ident_f).then_inc(ab_turned, 1)
            pe.wait_ge(abt_ready, 1)
            pe.wait_ge(hsum_ready, 1)

            def turn_mask(t, k):
                slot = (k % BODY) // 2
                pe.wait_ge(adj_loaded[slot], (t + k // BODY) * 16 + 16)
                pe.wait_ge(weights_ready, t * BODY + (CREDIT + k + 1 - RING))
                for j in range(2):
                    col = ((k % 2) * 2 + j) * P
                    for i in range(TILES):
                        last = nc.tensor.transpose(mask_t[:, k % RING, j * ROWS + i * P:j * ROWS + (i + 1) * P],
                                                   adj_sb[:, slot, i, col:col + P], ident_bf[:, :])
                last.then_inc(mask_ready, 1)

            def turn(c, t, b, first, final):
                for k in range(BODY):
                    turn_mask(t, k + LEAD)
                    pe.wait_ge(hi_ready, t * BODY + (CREDIT + k + 1))
                    wait_low_part(pe, t, k)
                    for i in range(TILES):
                        if first and k == 0:
                            pe.wait_ge(acc_free, c * TILES + (i + 1))
                        for j in range(2):
                            n = b * (2 * BODY) + (2 * k + j)
                            at = slice(j * ROWS + i * P, j * ROWS + (i + 1) * P)
                            begin = first and k == 0 and j == 0
                            end = final and k == BODY - 1 and j == 1
                            nc.tensor.matmul(acc[:, i, 0:FA], w_hi[:, k % RING, at], h_hi[:, n, :],
                                             start=begin, stop=False)
                            nc.tensor.matmul(acc[:, i, 0:F], w_hi[:, k % RING, at], h_lo[:, n, :],
                                             start=False, stop=False)
                            last = nc.tensor.matmul(acc[:, i, 0:FA], w_lo[:, k % RING, at], h_hi[:, n, :],
                                                    start=False, stop=end)
                        if final and k == BODY - 1 and i < TILES - 1:
                            last.then_inc(acc_done, 1)
                    last.then_inc(pair_done, 1)

            for k in range(LEAD):
                turn_mask(0, k)
            with pe.Fori(0, CHUNKS) as c:
                turn(c, c * BODIES, 0, True, False)
                with pe.Fori(1, BODIES - 1) as b:
                    turn(c, c * BODIES + b, b, False, False)
                turn(c, c * BODIES + (BODIES - 1), BODIES - 1, False, True)


_OUTS = [((N, F), "float32")]
_INS = ["x", "adj", "L0_gnn_W", "L0_gnn_a1", "L0_gnn_a2"]


def kernel(**inputs):
    import numpy as _np
    import concourse.bacc as _bacc
    from concourse import mybir as _mybir
    from concourse.bass_utils import run_bass_kernel_spmd as _run

    nc = _bacc.Bacc("TRN2", target_bir_lowering=False, num_devices=1)
    arrays, args = {}, []
    for name in _INS:
        a = _np.ascontiguousarray(inputs[name])
        arrays[f"in_{name}_dram"] = a
        args.append(nc.dram_tensor(f"in_{name}_dram", a.shape, _mybir.dt.from_np(a.dtype),
                                   kind="ExternalInput").ap())
    shape, dtype = _OUTS[0]
    args.append(nc.dram_tensor("out_0_dram", shape, _mybir.dt.from_np(_np.dtype(dtype)),
                               kind="ExternalOutput").ap())
    gat_kernel(nc, *args)
    r = _run(nc, [arrays], core_ids=[0])
    return r.results[0]["out_0_dram"]
```

```python
from contextlib import ExitStack

import concourse.bass as bass
from concourse import mybir

F32 = mybir.dt.float32
F32R = mybir.dt.float32r
BF16 = mybir.dt.bfloat16
I32 = mybir.dt.int32
ALU = mybir.AluOpType
ACT = mybir.ActivationFunctionType
AX = mybir.AxisListType

P = 128
N = 8192
F = 256
SLOPE = 0.2
EPS = 1e-5
SAFE = 30.0
LOWEST = -3.0e38
HIGHEST_EXPONENT = 60.0

TILES = 4
ROWS = TILES * P
CHUNKS = N // ROWS
BLOCKS = N // P
PAIRS = BLOCKS // 2
RING = 4
BODY = 8
BODIES = PAIRS // BODY
SLOTS = 4
COLS = N // (BODIES * SLOTS)
TOTAL = CHUNKS * BODIES
FA = F + 2
LEAD = 4
POOL_LO = (1, 3, 5, 7)
VEC_LO = tuple(k for k in range(BODY) if k not in POOL_LO)
CREDIT = RING
LO_CREDIT = BODY
assert BODY - 1 in POOL_LO and LEAD == RING


def gat_kernel(nc, x, adj, W, a1, a2, out):
    rows_dram = nc.dram_tensor("rows_scratch", (2, N), F32, kind="Internal").ap()
    dst_dram = nc.dram_tensor("dst_scratch", (N,), F32, kind="Internal").ap()

    adj_v = adj.rearrange("(c t p) (q n) -> c q p t n", c=CHUNKS, t=TILES, p=P, n=COLS)
    x_v = x.rearrange("(c t p) f -> c p t f", c=CHUNKS, t=TILES, p=P)
    out_v = out.rearrange("(c t p) f -> c p t f", c=CHUNKS, t=TILES, p=P)
    PIECE = ROWS
    PIECES = N // PIECE
    adj_rows_v = adj.rearrange("(t p) (q n) -> t q p n", p=P, n=PIECE)

    with ExitStack() as ctx:
        def sb(name, shape, dt):
            return ctx.enter_context(nc.sbuf_tensor(name, shape, dt))

        def sem(name):
            return ctx.enter_context(nc.semaphore(name))

        h_hi = sb("h_hi", [P, BLOCKS, FA], F32R)
        h_lo = sb("h_lo", [P, BLOCKS, F], F32R)
        adj_sb = sb("adj_sb", [P, SLOTS, TILES, COLS], BF16)
        w_hi = sb("w_hi", [P, RING, 2 * ROWS], F32R)
        w_lo = sb("w_lo", [P, RING, 2 * ROWS], F32R)
        weights = sb("weights", [P, RING, 2 * ROWS], F32)
        rows = sb("rows", [P, 2, ROWS], F32)
        xres = sb("xres", [P, TILES, F], F32)
        acc_sb = sb("acc_sb", [P, TILES, FA], F32)
        hsum = sb("hsum", [P, F], F32)
        ident_bf = sb("ident_bf", [P, P], BF16)
        src_dst = sb("src_dst", [P, 2, BLOCKS], F32)
        d_b = sb("d_b", [P, 2, BLOCKS], F32)
        top = sb("top", [P, 4], F32)
        top_all = sb("top_all", [P, 4], F32)
        shift = sb("shift", [P, 4], F32)
        unsafe = sb("unsafe", [P, 1], I32)
        row_stat = sb("row_stat", [P, 4, TILES], F32)
        bn = sb("bn", [P, TILES, 6], F32)
        mean_var = sb("mean_var", [P, TILES, 2], F32)

        w_t = acc_sb[:, 0:2, :]
        w_in = acc_sb[:, 2:4, 0:F]
        w_t_hi = h_hi[:, BLOCKS - 4:BLOCKS - 2, :]
        w_t_lo = h_hi[:, BLOCKS - 2:BLOCKS, :]
        ident_f = xres[:, 0, 0:P]
        ab_t = xres[:, 1, 0:P]
        ab = xres[:, 2, 0:P]
        a12 = xres[:, 3, 0:4].rearrange("p (o a) -> p o a", o=2)
        square = [xres[:, n, P:2 * P] for n in range(3)]
        x_sum = weights[:, 2, :]
        piece = acc_sb[:, :, :].rearrange("p t f -> p (t f)")

        t_ps = ctx.enter_context(nc.psum_tensor("t_ps", [P, RING, 512], F32))
        acc = ctx.enter_context(nc.psum_tensor("acc", [P, TILES, 512], F32))
        mask_t = t_ps[:, :, :].bitcast(BF16)

        wa_loaded = sem("wa_loaded")
        ident_step = sem("ident_step")
        ident_ready = sem("ident_ready")
        w_turned = sem("w_turned")
        x_loaded = [sem(f"x_loaded{i}") for i in range(2)]
        x_turned = sem("x_turned")
        xt_hi_ready = sem("xt_hi_ready")
        xt_lo_ready = sem("xt_lo_ready")
        h_ready = sem("h_ready")
        h_hi_ready = sem("h_hi_ready")
        h_lo_ready = sem("h_lo_ready")
        sd_ready = sem("sd_ready")
        constants_ready = sem("constants_ready")
        w_parts_ready = sem("w_parts_ready")
        x_summed = sem("x_summed")
        x_sum_turned = sem("x_sum_turned")
        x_sum_ready = sem("x_sum_ready")
        setup_step = sem("setup_step")
        general_step = sem("general_step")
        piece_step = sem("piece_step")
        exponent_step = sem("exponent_step")
        norm_step = sem("norm_step")
        norm_end_step = sem("norm_end_step")
        waited = sem("waited")
        top_ready = sem("top_ready")
        top_all_ready = sem("top_all_ready")
        flag_ready = sem("flag_ready")
        ab_ready = sem("ab_ready")
        db_ready = sem("db_ready")
        ab_turned = sem("ab_turned")
        first_rows_turned = sem("first_rows_turned")
        first_rows_ready = sem("first_rows_ready")
        abt_ready = sem("abt_ready")
        rows_written = sem("rows_written")
        hsum_done = sem("hsum_done")
        hsum_ready = sem("hsum_ready")
        dst_written = sem("dst_written")
        piece_loaded = sem("piece_loaded")
        piece_used = sem("piece_used")
        exponent_ready = sem("exponent_ready")
        adj_loaded = [sem(f"adj_loaded{i}") for i in range(SLOTS)]
        rows_loaded = sem("rows_loaded")
        mask_ready = sem("mask_ready")
        bare_ready = sem("bare_ready")
        weights_ready = sem("weights_ready")
        hi_ready = sem("hi_ready")
        lo_vec = sem("lo_vec")
        lo_pool = sem("lo_pool")
        pair_done = sem("pair_done")
        acc_done = sem("acc_done")
        acc_free = sem("acc_free")
        acc_used = sem("acc_used")
        xres_loaded = sem("xres_loaded")
        var_ready = sem("var_ready")
        std_ready = sem("std_ready")
        out_ready = sem("out_ready")
        out_written = sem("out_written")

        def low_part_count(k):
            made, s = (POOL_LO, lo_pool) if k % BODY in POOL_LO else (VEC_LO, lo_vec)
            return s, len(made), made.index(k % BODY) + 1 + len(made) * (k // BODY)

        def wait_low_part(eng, turn, k):
            s, per_turn, rank = low_part_count(k)
            eng.wait_ge(s, turn * per_turn + (LO_CREDIT + rank))

        def chain(eng, step, start):
            made = [0]

            def link(instruction):
                made[0] += 1
                instruction.then_inc(step, 1)
                eng.wait_ge(step, start + made[0])
            return link

        block = ctx.enter_context(nc.Block())

        @block.sync
        def _(sp):
            sp.dma_start(w_in, W.rearrange("(o p) k -> p o k", p=P)).then_inc(wa_loaded, 16)
            with nc.allow_non_contiguous_dma(reason="256 words each"):
                sp.dma_start(a12[:, :, 0], a1.rearrange("(o p) -> p o", p=P)).then_inc(wa_loaded, 16)
                sp.dma_start(a12[:, :, 1], a2.rearrange("(o p) -> p o", p=P)).then_inc(wa_loaded, 16)
            for g in range(2):
                sp.dma_start(weights[:, g, :].rearrange("p (t f) -> p t f", t=TILES),
                             x_v[g]).then_inc(x_loaded[g], 16)
            with sp.Fori(0, CHUNKS // 2 - 1) as u:
                for g in range(2):
                    sp.wait_ge(x_summed, u * 2 + (g + 2))
                    sp.dma_start(weights[:, g, :].rearrange("p (t f) -> p t f", t=TILES),
                                 x_v[u * 2 + (g + 2)]).then_inc(x_loaded[g], 16)
            sp.wait_ge(abt_ready, 1)
            sp.dma_start(rows_dram.rearrange("a (t p) -> (a t) p", p=P), ab_t).then_inc(rows_written, 16)
            sp.wait_ge(rows_written, 16)

            def load_rows(chunk):
                for a in range(2):
                    src = rows_dram[a:a + 1, bass.ds(chunk * ROWS, ROWS)]
                    sp.dma_start(rows[:, a, :], src.to_broadcast([P, ROWS])).then_inc(rows_loaded, 16)

            sp.wait_ge(x_turned, CHUNKS)
            sp.dma_start(xres[:, :, :], x_v[0]).then_inc(xres_loaded, 16)

            def serve(c, more):
                sp.wait_ge(bare_ready, c * PAIRS + PAIRS)
                load_rows(c + 1 if more else 0)
                sp.wait_ge(out_ready, c + 1)
                sp.dma_start(out_v[c], xres[:, :, :]).then_inc(out_written, 16)
                sp.wait_ge(out_written, c * 16 + 16)
                if more:
                    sp.dma_start(xres[:, :, :], x_v[c + 1]).then_inc(xres_loaded, 16)

            with sp.Fori(0, CHUNKS - 1) as c:
                serve(c, True)
            serve(CHUNKS - 1, False)

        @block.gpsimd
        def _(pool):
            nc.gpsimd.memset(ident_bf[:, :], 0.0).then_inc(ident_step, 1)
            nc.gpsimd.memset(ident_f, 0.0).then_inc(ident_step, 1)
            pool.wait_ge(ident_step, 2)
            for m in (ident_bf[:, :], ident_f):
                nc.gpsimd.affine_select(out=m, in_=m, compare_op=ALU.not_equal, fill=1.0, base=0,
                                        pattern=[[-1, P]], channel_multiplier=1).then_inc(ident_ready, 1)
            nc.gpsimd.memset(x_sum, 0.0).then_inc(x_summed, 1)

            for s in range(SLOTS):
                pool.dma_start(adj_sb[:, s, :, :], adj_v[0, s]).then_inc(adj_loaded[s], 16)
            with pool.Fori(0, CHUNKS // 2) as u:
                for g in range(2):
                    pool.wait_ge(x_turned, u * 2 + (g + 1))
                    pool.wait_ge(x_summed, u * 2 + (g + 1))
                    nc.gpsimd.tensor_tensor(x_sum, x_sum, weights[:, g, :], ALU.add).then_inc(x_summed, 1)
            pool.wait_ge(top_ready, 1)
            nc.gpsimd.partition_all_reduce(top_all[:, :], top[:, :], P,
                                           bass.bass_isa.ReduceOp.max).then_inc(top_all_ready, 1)
            pool.sem_inc(lo_pool, LO_CREDIT)

            def turn(t, refill):
                for k in range(BODY):
                    if k in POOL_LO:
                        pool.wait_ge(hi_ready, t * BODY + (CREDIT + k + 1))
                        pool.wait_ge(pair_done, t * BODY + (CREDIT + k + 1 - RING))
                        nc.gpsimd.tensor_tensor(w_lo[:, k % RING, :], weights[:, k % RING, :],
                                                w_hi[:, k % RING, :].bitcast(F32),
                                                ALU.subtract).then_inc(lo_pool, 1)
                    if k % 2 == 0:
                        continue
                    if refill:
                        nxt = t + 1
                        pool.wait_ge(mask_ready, t * BODY + (k + 1))
                        pool.dma_start(adj_sb[:, k // 2, :, :],
                                       adj_v[nxt // BODIES, (nxt % BODIES) * SLOTS + k // 2]
                                       ).then_inc(adj_loaded[k // 2], 16)
                    elif k < LEAD:
                        pool.wait_ge(mask_ready, t * BODY + (k + 1))
                        pool.dma_start(adj_sb[:, k // 2, 0, 0:P],
                                       adj_v[0, k // 2][:, 0, 0:P]).then_inc(adj_loaded[k // 2], 16)

            with pool.Fori(0, TOTAL - 1) as t:
                turn(t, True)
            turn(TOTAL - 1, False)

        def act_split_x(g, n):
            nc.scalar.wait_ge(x_turned, g + 1)
            for half in range(2):
                last = nc.scalar.copy(w_hi[:, n, half * 512:(half + 1) * 512], t_ps[:, 2 * (n % 2) + half, :])
            last.then_inc(xt_hi_ready, 1)

        def act_split_h(g):
            for t in range(TILES):
                nc.scalar.wait_ge(h_ready, g * TILES + (t + 1))
                nc.scalar.copy(h_hi[:, g * TILES + t, 0:F], acc[:, t, 0:F]).then_inc(h_hi_ready, 1)

        def act_main(act, general):
            act.sem_inc(hi_ready, CREDIT)
            if not general:
                nc.scalar.preload_act_table(ACT.Sqrt)

            def exponential(s, count):
                act.wait_ge(exponent_ready, count)
                nc.scalar.activation(weights[:, s, :], weights[:, s, :], ACT.Exp).then_inc(bare_ready, 1)

            def high_part(t, k):
                act.wait_ge(weights_ready, t * BODY + (CREDIT + k + 1))
                act.wait_ge(pair_done, t * BODY + (CREDIT + k + 1 - RING))
                nc.scalar.copy(w_hi[:, k % RING, :], weights[:, k % RING, :]).then_inc(hi_ready, 1)
                if general:
                    exponential((k + 1) % RING, t * BODY + (k + 2))

            def evict(c):
                act.wait_ge(acc_used, c + 1)
                for t in range(TILES):
                    if t < TILES - 1:
                        act.wait_ge(acc_done, c * (TILES - 1) + (t + 1))
                    else:
                        act.wait_ge(pair_done, c * PAIRS + (PAIRS + CREDIT))
                    nc.scalar.copy(acc_sb[:, t, :], acc[:, t, 0:FA]).then_inc(acc_free, 1)

            def deviation(c):
                act.wait_ge(var_ready, c + 1)
                nc.scalar.activation(row_stat[:, 3, :], row_stat[:, 2, :], ACT.Sqrt).then_inc(std_ready, 1)

            def first_turn(c, epilogue):
                for k in range(BODY):
                    high_part(c * BODIES, k)
                    if epilogue and k == 2:
                        evict(c - 1)
                    if epilogue and k == 5:
                        deviation(c - 1)

            def other_turns(c):
                with act.Fori(1, BODIES) as b:
                    for k in range(BODY):
                        high_part(c * BODIES + b, k)

            if general:
                exponential(0, 1)
            first_turn(0, False)
            other_turns(0)
            with act.Fori(1, CHUNKS) as c:
                first_turn(c, True)
                other_turns(c)
            evict(CHUNKS - 1)
            deviation(CHUNKS - 1)

        @block.scalar
        def _(act):
            act.sem_inc(acc_free, TILES)
            nc.scalar.preload_act_table(ACT.Exp)
            act_split_x(0, 0)
            with act.Fori(0, CHUNKS // 4 - 1) as u:
                for n in range(4):
                    act_split_x(u * 4 + (n + 1), (n + 1) % 4)
                    act_split_h(u * 4 + n)
            for n in range(CHUNKS - 4, CHUNKS - 1):
                act_split_x(n + 1, (n + 1) % 4)
                act_split_h(n)
            act.wait_ge(sd_ready, BLOCKS)
            act_split_h(CHUNKS - 1)
            act.wait_ge(flag_ready, 1)
            flag = act.value_load(unsafe[0:1, 0:1], min_val=0, max_val=1)
            with act.If(flag < 1):
                nc.scalar.activation(ab[:, 0:BLOCKS], src_dst[:, 0, :], ACT.Exp, bias=shift[:, 2:3],
                                     scale=SLOPE - 1.0).then_inc(ab_ready, 1)
                nc.scalar.activation(d_b[:, 1, :], src_dst[:, 1, :], ACT.Exp, bias=shift[:, 0:1], scale=1.0)
                nc.scalar.activation(d_b[:, 0, :], src_dst[:, 1, :], ACT.Exp, bias=shift[:, 1:2],
                                     scale=SLOPE).then_inc(db_ready, 1)
            with act.Else():
                act.wait_ge(hsum_ready, 1)
                with nc.allow_non_contiguous_dma(reason="a table of 8192 words, once"):
                    act.dma_start(dst_dram.rearrange("(t p) -> p t", p=P),
                                  src_dst[:, 1, :]).then_inc(dst_written, 16)
                act.wait_ge(dst_written, 16)
                with act.Fori(0, BLOCKS) as t:
                    with act.Fori(0, PIECES) as q:
                        act.wait_ge(piece_used, t * PIECES + (q + 1))
                        act.dma_start(piece[:, 0:PIECE].bitcast(I32), adj_rows_v[t, q]).then_inc(piece_loaded, 16)
                        act.dma_start(piece[:, PIECE:2 * PIECE],
                                      dst_dram.rearrange("(a n) -> a n", a=1)[:, bass.ds(q * PIECE, PIECE)]
                                      .to_broadcast([P, PIECE])).then_inc(piece_loaded, 16)
            act.wait_ge(first_rows_turned, 1)
            nc.scalar.copy(rows[:, :, :], t_ps[:, 1:3, :]).then_inc(first_rows_ready, 1)
            act.wait_ge(ab_turned, 1)
            nc.scalar.copy(ab_t, t_ps[:, 0, 0:P]).then_inc(abt_ready, 1)
            with act.If(flag < 1):
                act_main(act, False)
            with act.Else():
                act_main(act, True)

        def vec_main(dve, general):
            dve.sem_inc(weights_ready, CREDIT)
            dve.sem_inc(lo_vec, LO_CREDIT)
            dve.sem_inc(acc_used, 1)

            def bare(c, t, k, col):
                s = k % RING
                dve.wait_ge(hi_ready, t * BODY + (CREDIT + k + 1 - RING))
                wait_low_part(dve, t, k - RING)
                link = chain(dve, exponent_step, (t * BODY + k) * 4)
                for j in range(2):
                    w = weights[:, s, j * ROWS:(j + 1) * ROWS]
                    if not general:
                        last = nc.vector.tensor_scalar(w, rows[:, 0, :], d_b[:, 0, bass.ds(col + j, 1)],
                                                       d_b[:, 1, bass.ds(col + j, 1)], ALU.mult, ALU.max)
                        continue
                    link(nc.vector.tensor_scalar(w, rows[:, 1, :], d_b[:, 0, bass.ds(col + j, 1)], None, ALU.add))
                    link(nc.vector.scalar_tensor_tensor(w, rows[:, 0, :], src_dst[:, 1, bass.ds(col + j, 1)], w,
                                                        ALU.add, ALU.max))
                    last = nc.vector.tensor_scalar(w, w, HIGHEST_EXPONENT, None, ALU.min)
                last.then_inc(exponent_ready if general else bare_ready, 1)

            def masked(t, k):
                dve.wait_ge(bare_ready, t * BODY + (k + 1))
                dve.wait_ge(mask_ready, t * BODY + (k + 1))
                nc.vector.scalar_tensor_tensor(weights[:, k % RING, :], mask_t[:, k % RING, :], 0.0,
                                               weights[:, k % RING, :], ALU.not_equal,
                                               ALU.mult).then_inc(weights_ready, 1)

            def low_part(t, k):
                dve.wait_ge(hi_ready, t * BODY + (CREDIT + k + 1))
                dve.wait_ge(pair_done, t * BODY + (CREDIT + k + 1 - RING))
                nc.vector.tensor_tensor(w_lo[:, k % RING, :], weights[:, k % RING, :],
                                        w_hi[:, k % RING, :].bitcast(F32), ALU.subtract).then_inc(lo_vec, 1)

            def step(c, t, b, k):
                masked(t, k)
                if k >= 1 and (k - 1) in VEC_LO:
                    low_part(t, k - 1)
                if k + 1 < BODY:
                    bare(c, t, k + 1, b * (2 * BODY) + 2 * (k + 1))

            def start_next(c, t, b):
                bare(c, t + 1, 0, (b + 1) * (2 * BODY))

            def norm_sums(c):
                dve.wait_ge(acc_free, c * TILES + 2 * TILES)
                dve.wait_ge(xres_loaded, c * 16 + 16)
                link = chain(dve, norm_step, c * 6)
                den = acc_sb[:, :, F]
                link(nc.vector.tensor_scalar(row_stat[:, 0, :], den, 0.0, None, ALU.is_equal))
                link(nc.vector.scalar_tensor_tensor(row_stat[:, 1, :], row_stat[:, 0, :], float(N), den,
                                                    ALU.mult, ALU.add))
                link(nc.vector.reciprocal(row_stat[:, 1, :], row_stat[:, 1, :]))
                for t in range(TILES):
                    last = nc.vector.scalar_tensor_tensor(acc_sb[:, t, 0:F], hsum[:, :], row_stat[:, 0, t:t + 1],
                                                          acc_sb[:, t, 0:F], ALU.mult, ALU.add)
                link(last)
                for t in range(TILES):
                    last = nc.vector.scalar_tensor_tensor(xres[:, t, :], acc_sb[:, t, 0:F], row_stat[:, 1, t:t + 1],
                                                          xres[:, t, :], ALU.mult, ALU.add)
                last.then_inc(acc_used, 1)
                dve.wait_ge(acc_used, c + 2)
                for t in range(TILES):
                    last = nc.vector.bn_stats(bn[:, t, :], xres[:, t, :])
                link(last)
                dve.sem_inc(waited, 1)
                for t in range(TILES):
                    last = nc.vector.bn_aggr(mean_var[:, t, :], bn[:, t, :])
                link(last)
                nc.vector.tensor_scalar(row_stat[:, 2, :], mean_var[:, :, 1], EPS, None,
                                        ALU.add).then_inc(var_ready, 1)

            def normalise(c):
                dve.wait_ge(std_ready, c + 1)
                link = chain(dve, norm_end_step, c)
                link(nc.vector.reciprocal(row_stat[:, 3, :], row_stat[:, 3, :]))
                for t in range(TILES):
                    last = nc.vector.tensor_scalar(xres[:, t, :], xres[:, t, :], mean_var[:, t, 0:1],
                                                   row_stat[:, 3, t:t + 1], ALU.subtract, ALU.mult)
                last.then_inc(out_ready, 1)

            def first_turn(c, epilogue):
                for k in range(BODY):
                    step(c, c * BODIES, 0, k)
                    if epilogue and k == 4:
                        norm_sums(c - 1)
                    if epilogue and k == 6:
                        normalise(c - 1)
                start_next(c, c * BODIES, 0)

            def other_turns(c):
                with dve.Fori(1, BODIES - 1) as b:
                    for k in range(BODY):
                        step(c, c * BODIES + b, b, k)
                    start_next(c, c * BODIES + b, b)
                b = BODIES - 1
                for k in range(BODY):
                    step(c, c * BODIES + b, b, k)
                dve.wait_ge(rows_loaded, c * 32 + 32)
                bare(c + 1, c * BODIES + BODIES, 0, 0)

            dve.wait_ge(first_rows_ready, 1)
            bare(0, 0, 0, 0)
            first_turn(0, False)
            other_turns(0)
            with dve.Fori(1, CHUNKS) as c:
                first_turn(c, True)
                other_turns(c)
            norm_sums(CHUNKS - 1)
            normalise(CHUNKS - 1)

        @block.vector
        def _(dve):
            link = chain(dve, setup_step, 0)
            dve.sem_inc(h_lo_ready, TILES)
            dve.sem_inc(xt_lo_ready, 1)
            nc.vector.memset(square[0], 1.0).then_inc(constants_ready, 1)
            dve.wait_ge(w_turned, 1)
            nc.vector.tensor_copy(w_t[:, :, 0:F], t_ps[:, 2, :].rearrange("p (k o) -> p k o", k=2))
            link(nc.vector.tensor_copy(w_t[:, :, F:FA], t_ps[:, 3, 0:4].rearrange("p (k a) -> p k a", k=2)))
            link(nc.vector.tensor_copy(w_t_hi, w_t))
            nc.vector.tensor_tensor(w_t_lo, w_t, w_t_hi.bitcast(F32), ALU.subtract).then_inc(w_parts_ready, 1)
            nc.vector.memset(h_hi[:, 0:BLOCKS - 4, F:F + 1].bitcast(F32), 1.0)
            nc.vector.memset(h_hi[:, 0:BLOCKS - 4, F + 1:FA].bitcast(F32), 0.0)

            def split_x(g, n):
                dve.wait_ge(xt_hi_ready, g + 1)
                for half in range(2):
                    at = slice(half * 512, (half + 1) * 512)
                    last = nc.vector.tensor_tensor(w_lo[:, n, at], t_ps[:, 2 * (n % 2) + half, :],
                                                   w_hi[:, n, at].bitcast(F32), ALU.subtract)
                last.then_inc(xt_lo_ready, 1)

            def split_h(g, dots=True):
                for t in range(TILES):
                    n = g * TILES + t
                    dve.wait_ge(h_hi_ready, n + 1)
                    if dots:
                        nc.vector.tensor_copy(src_dst[:, :, bass.ds(n, 1)],
                                              acc[:, t, F:FA].rearrange("p (a o) -> p a o", o=1)
                                              ).then_inc(sd_ready, 1)
                    nc.vector.tensor_tensor(h_lo[:, n, :], acc[:, t, 0:F], h_hi[:, n, 0:F].bitcast(F32),
                                            ALU.subtract).then_inc(h_lo_ready, 1)

            split_x(0, 0)
            with dve.Fori(0, CHUNKS // 4 - 1) as u:
                for n in range(4):
                    split_x(u * 4 + (n + 1), (n + 1) % 4)
                    split_h(u * 4 + n)
            for n in range(CHUNKS - 4, CHUNKS - 1):
                split_x(n + 1, (n + 1) % 4)
                split_h(n)
            dve.wait_ge(h_ready, BLOCKS)
            nc.vector.tensor_copy(src_dst[:, :, BLOCKS - TILES:BLOCKS],
                                  acc[:, :, F:FA].rearrange("p t a -> p a t")).then_inc(sd_ready, TILES)
            dve.wait_ge(sd_ready, BLOCKS)
            link(nc.vector.tensor_scalar(d_b[:, :, :], src_dst[:, :, :], -1.0, None, ALU.mult))
            nc.vector.reduce_max(top[:, 0:2], src_dst[:, :, :], AX.X)
            nc.vector.reduce_max(top[:, 2:4], d_b[:, :, :], AX.X).then_inc(top_ready, 1)
            dve.wait_ge(x_sum_turned, 1)
            nc.vector.tensor_copy(xres[:, 1:3, P:2 * P],
                                  t_ps[:, 2, 0:2 * P].rearrange("p (k n) -> p k n", k=2)).then_inc(x_sum_ready, 1)
            dve.wait_ge(top_all_ready, 1)
            for n, factor in enumerate((-1.0, -SLOPE, SLOPE - 1.0)):
                nc.vector.tensor_scalar(shift[:, n:n + 1], top_all[:, 1:2], factor, None, ALU.mult)
            link(nc.vector.reduce_max(shift[:, 3:4], top_all[:, :], AX.X))
            nc.vector.tensor_scalar(unsafe[:, :], shift[:, 3:4], SAFE, None, ALU.is_gt).then_inc(flag_ready, 1)
            split_h(CHUNKS - 1, dots=False)
            dve.wait_ge(hsum_done, 1)
            nc.vector.tensor_copy(hsum[:, :], t_ps[:, 3, 0:F]).then_inc(hsum_ready, 1)
            dve.wait_ge(flag_ready, 1)
            flag = dve.value_load(unsafe[0:1, 0:1], min_val=0, max_val=1)
            with dve.If(flag < 1):
                nc.vector.memset(ab[:, BLOCKS:2 * BLOCKS], 0.0).then_inc(ab_ready, 1)
            with dve.Else():
                link = chain(dve, general_step, 0)
                link(nc.vector.memset(ab[:, BLOCKS:2 * BLOCKS], LOWEST))
                dve.sem_inc(piece_used, 1)
                with dve.Fori(0, BLOCKS) as t:
                    with dve.Fori(0, PIECES) as q:
                        link = chain(dve, piece_step, (t * PIECES + q) * 3)
                        link(nc.vector.memset(t_ps[:, 1, :], LOWEST))
                        dve.wait_ge(piece_loaded, (t * PIECES + q) * 32 + 32)
                        dve.sem_inc(waited, 1)
                        link(nc.vector.copy_predicated(t_ps[:, 1, :], piece[:, 0:PIECE].bitcast(I32),
                                                       piece[:, PIECE:2 * PIECE]))
                        link(nc.vector.reduce_max(shift[:, 0:1], t_ps[:, 1, :], AX.X))
                        nc.vector.tensor_tensor(ab[:, bass.ds(t + BLOCKS, 1)], ab[:, bass.ds(t + BLOCKS, 1)],
                                                shift[:, 0:1], ALU.max).then_inc(piece_used, 1)
                dve.wait_ge(piece_used, BLOCKS * PIECES + 1)
                link = chain(dve, general_step, 1)
                m, a, s = ab[:, BLOCKS:2 * BLOCKS], ab[:, 0:BLOCKS], src_dst[:, 0, :]
                link(nc.vector.tensor_tensor(m, m, s, ALU.add))
                link(nc.vector.scalar_tensor_tensor(m, m, SLOPE, m, ALU.mult, ALU.max))
                link(nc.vector.tensor_tensor(a, s, m, ALU.subtract))
                link(nc.vector.scalar_tensor_tensor(m, s, SLOPE, m, ALU.mult, ALU.subtract))
                link(nc.vector.tensor_scalar(d_b[:, 0, :], src_dst[:, 1, :], SLOPE, None, ALU.mult))
                dve.sem_inc(ab_ready, 2)
            nc.vector.memset(h_hi[:, BLOCKS - 4:BLOCKS, F:F + 1].bitcast(F32), 1.0)
            nc.vector.memset(h_hi[:, BLOCKS - 4:BLOCKS, F + 1:FA].bitcast(F32), 0.0).then_inc(constants_ready, 1)
            with dve.If(flag < 1):
                dve.wait_ge(db_ready, 1)
                vec_main(dve, False)
            with dve.Else():
                vec_main(dve, True)

        @block.tensor
        def _(pe):
            pe.sem_inc(pair_done, CREDIT)
            pe.wait_ge(ident_ready, 2)
            pe.wait_ge(wa_loaded, 48)
            for k in range(2):
                for o in range(2):
                    nc.tensor.transpose(t_ps[:, 2, k * F + o * P:k * F + (o + 1) * P],
                                        w_in[:, o, k * P:(k + 1) * P], ident_f)
            for k in range(2):
                for o in range(2):
                    last = nc.tensor.matmul(t_ps[:, 3, 2 * k:2 * k + 2], w_in[:, o, k * P:(k + 1) * P],
                                            a12[:, o, :], start=(o == 0), stop=(o == 1))
            last.then_inc(w_turned, 1)

            def turn_x(u, n):
                pe.wait_ge(x_loaded[n % 2], (u * 2 + n // 2) * 16 + 16)
                pe.wait_ge(xt_lo_ready, u * 4 + n)
                for t in range(TILES):
                    for k in range(2):
                        m = (t % 2) * 2 + k
                        last = nc.tensor.transpose(t_ps[:, 2 * (n % 2) + t // 2, m * P:(m + 1) * P],
                                                   weights[:, n % 2, t * F + k * P:t * F + (k + 1) * P], ident_f)
                last.then_inc(x_turned, 1)

            def product(out, n, t):
                for k in range(2):
                    at = slice((t * 2 + k) * P, (t * 2 + k + 1) * P)
                    nc.tensor.matmul(out, w_hi[:, n, at], w_t_hi[:, k, :], start=(k == 0), stop=False)
                    nc.tensor.matmul(out, w_hi[:, n, at], w_t_lo[:, k, :], start=False, stop=False)
                    last = nc.tensor.matmul(out, w_lo[:, n, at], w_t_hi[:, k, :], start=False, stop=(k == 1))
                return last

            def make_h(g, n):
                pe.wait_ge(xt_lo_ready, g + 2)
                for t in range(TILES):
                    pe.wait_ge(h_lo_ready, g * TILES + (t + 1))
                    product(acc[:, t, 0:FA], n, t).then_inc(h_ready, 1)

            turn_x(0, 0)
            pe.wait_ge(w_parts_ready, 1)
            with pe.Fori(0, CHUNKS // 4 - 1) as u:
                for n in range(4):
                    turn_x(u, n + 1)
                    make_h(u * 4 + n, n)
            for n in range(4):
                if n < 3:
                    turn_x(CHUNKS // 4 - 1, n + 1)
                make_h(CHUNKS - 4 + n, n)
            pe.wait_ge(x_summed, CHUNKS + 1)
            pe.wait_ge(constants_ready, 1)
            for k in range(2):
                for t in range(TILES):
                    last = nc.tensor.matmul(t_ps[:, 2, k * P:(k + 1) * P],
                                            x_sum[:, t * F + k * P:t * F + (k + 1) * P], square[0],
                                            start=(t == 0), stop=(t == TILES - 1))
            last.then_inc(x_sum_turned, 1)
            pe.wait_ge(x_sum_ready, 1)
            for k in range(2):
                last = nc.tensor.matmul(t_ps[:, 3, 0:F], square[1 + k], w_t[:, k, 0:F], start=(k == 0), stop=(k == 1))
            last.then_inc(hsum_done, 1)
            pe.wait_ge(ab_ready, 2)
            for a in range(2):
                for t in range(TILES):
                    last = nc.tensor.matmul(t_ps[:, 1 + a, t * P:(t + 1) * P],
                                            ab[:, a * BLOCKS + t:a * BLOCKS + t + 1].to_broadcast([P, P]),
                                            ident_f, start=True, stop=True)
            last.then_inc(first_rows_turned, 1)
            nc.tensor.transpose(t_ps[:, 0, 0:P], ab, ident_f).then_inc(ab_turned, 1)
            pe.wait_ge(abt_ready, 1)
            pe.wait_ge(hsum_ready, 1)

            def turn_mask(t, k):
                slot = (k % BODY) // 2
                if k % 2 == 0:
                    pe.wait_ge(adj_loaded[slot], (t + k // BODY) * 16 + 16)
                for j in range(2):
                    col = ((k % 2) * 2 + j) * P
                    for i in range(TILES):
                        last = nc.tensor.transpose(mask_t[:, k % RING, j * ROWS + i * P:j * ROWS + (i + 1) * P],
                                                   adj_sb[:, slot, i, col:col + P], ident_bf[:, :])
                last.then_inc(mask_ready, 1)

            def turn(c, t, b, first, final):
                for k in range(BODY):
                    pe.wait_ge(hi_ready, t * BODY + (CREDIT + k + 1))
                    turn_mask(t, k + LEAD)
                    wait_low_part(pe, t, k)
                    for i in range(TILES):
                        if first and k == 0:
                            pe.wait_ge(acc_free, c * TILES + (i + 1))
                        for j in range(2):
                            n = b * (2 * BODY) + (2 * k + j)
                            at = slice(j * ROWS + i * P, j * ROWS + (i + 1) * P)
                            begin = first and k == 0 and j == 0
                            end = final and k == BODY - 1 and j == 1
                            nc.tensor.matmul(acc[:, i, 0:FA], w_hi[:, k % RING, at], h_hi[:, n, :],
                                             start=begin, stop=False)
                            nc.tensor.matmul(acc[:, i, 0:F], w_hi[:, k % RING, at], h_lo[:, n, :],
                                             start=False, stop=False)
                            last = nc.tensor.matmul(acc[:, i, 0:FA], w_lo[:, k % RING, at], h_hi[:, n, :],
                                                    start=False, stop=end)
                        if final and k == BODY - 1 and i < TILES - 1:
                            last.then_inc(acc_done, 1)
                    last.then_inc(pair_done, 1)

            for k in range(LEAD):
                turn_mask(0, k)
            pe.wait_ge(h_lo_ready, BLOCKS + TILES)
            pe.wait_ge(constants_ready, 2)
            with pe.Fori(0, CHUNKS) as c:
                turn(c, c * BODIES, 0, True, False)
                with pe.Fori(1, BODIES - 1) as b:
                    turn(c, c * BODIES + b, b, False, False)
                turn(c, c * BODIES + (BODIES - 1), BODIES - 1, False, True)


_OUTS = [((N, F), "float32")]
_INS = ["x", "adj", "L0_gnn_W", "L0_gnn_a1", "L0_gnn_a2"]


def kernel(**inputs):
    import numpy as _np
    import concourse.bacc as _bacc
    from concourse import mybir as _mybir
    from concourse.bass_utils import run_bass_kernel_spmd as _run

    nc = _bacc.Bacc("TRN2", target_bir_lowering=False, num_devices=1)
    arrays, args = {}, []
    for name in _INS:
        a = _np.ascontiguousarray(inputs[name])
        arrays[f"in_{name}_dram"] = a
        args.append(nc.dram_tensor(f"in_{name}_dram", a.shape, _mybir.dt.from_np(a.dtype),
                                   kind="ExternalInput").ap())
    shape, dtype = _OUTS[0]
    args.append(nc.dram_tensor("out_0_dram", shape, _mybir.dt.from_np(_np.dtype(dtype)),
                               kind="ExternalOutput").ap())
    gat_kernel(nc, *args)
    r = _run(nc, [arrays], core_ids=[0])
    return r.results[0]["out_0_dram"]
```

```python
from contextlib import ExitStack

import concourse.bass as bass
from concourse import mybir

F32 = mybir.dt.float32
F32R = mybir.dt.float32r
BF16 = mybir.dt.bfloat16
I32 = mybir.dt.int32
ALU = mybir.AluOpType
ACT = mybir.ActivationFunctionType
AX = mybir.AxisListType

P = 128
N = 8192
F = 256
SLOPE = 0.2
EPS = 1e-5
SAFE = 30.0
LOWEST = -3.0e38
HIGHEST_EXPONENT = 60.0

TILES = 4
ROWS = TILES * P
CHUNKS = N // ROWS
BLOCKS = N // P
PAIRS = BLOCKS // 2
RING = 4
BODY = 8
BODIES = PAIRS // BODY
SLOTS = 4
COLS = N // (BODIES * SLOTS)
TOTAL = CHUNKS * BODIES
FA = F + 2
TAIL = 2
HALF = TILES // 2
LEAD = 4
POOL_LO = (1, 3, 5, 7)
VEC_LO = tuple(k for k in range(BODY) if k not in POOL_LO)
CREDIT = RING
LO_CREDIT = BODY
assert BODY - 1 in POOL_LO and LEAD == RING


def gat_kernel(nc, x, adj, W, a1, a2, out):
    rows_dram = nc.dram_tensor("rows_scratch", (2, N), F32, kind="Internal").ap()
    dst_dram = nc.dram_tensor("dst_scratch", (N,), F32, kind="Internal").ap()

    adj_v = adj.rearrange("(c t p) (q n) -> c q p t n", c=CHUNKS, t=TILES, p=P, n=COLS)
    x_v = x.rearrange("(c t p) f -> c p t f", c=CHUNKS, t=TILES, p=P)
    out_v = out.rearrange("(c t p) f -> c p t f", c=CHUNKS, t=TILES, p=P)
    PIECE = ROWS
    PIECES = N // PIECE
    adj_rows_v = adj.rearrange("(t p) (q n) -> t q p n", p=P, n=PIECE)

    with ExitStack() as ctx:
        def sb(name, shape, dt):
            return ctx.enter_context(nc.sbuf_tensor(name, shape, dt))

        def sem(name):
            return ctx.enter_context(nc.semaphore(name))

        h_hi = sb("h_hi", [P, BLOCKS, FA], F32R)
        h_lo = sb("h_lo", [P, BLOCKS, F], F32R)
        adj_sb = sb("adj_sb", [P, SLOTS, TILES, COLS], BF16)
        w_hi = sb("w_hi", [P, RING, 2 * ROWS], F32R)
        w_lo = sb("w_lo", [P, RING, 2 * ROWS], F32R)
        weights = sb("weights", [P, RING, 2 * ROWS], F32)
        rows = sb("rows", [P, 2, ROWS], F32)
        xres = sb("xres", [P, TILES, F], F32)
        acc_sb = sb("acc_sb", [P, TILES, FA], F32)
        hsum = sb("hsum", [P, F], F32)
        ident_bf = sb("ident_bf", [P, P], BF16)
        src_dst = sb("src_dst", [P, 2, BLOCKS], F32)
        d_b = sb("d_b", [P, 2, BLOCKS], F32)
        top = sb("top", [P, 4], F32)
        top_all = sb("top_all", [P, 4], F32)
        shift = sb("shift", [P, 4], F32)
        unsafe = sb("unsafe", [P, 1], I32)
        row_stat = sb("row_stat", [P, 4, TILES], F32)
        bn = sb("bn", [P, TILES, 6], F32)
        mean_var = sb("mean_var", [P, TILES, 2], F32)

        w_t = acc_sb[:, 0:2, :]
        w_in = acc_sb[:, 2:4, 0:F]
        w_t_hi = h_hi[:, BLOCKS - 4:BLOCKS - 2, :]
        w_t_lo = h_hi[:, BLOCKS - 2:BLOCKS, :]
        ident_f = xres[:, 0, 0:P]
        ab_t = xres[:, 1, 0:P]
        ab = xres[:, 2, 0:P]
        a12 = xres[:, 3, 0:4].rearrange("p (o a) -> p o a", o=2)
        square = [xres[:, n, P:2 * P] for n in range(3)]
        x_sum = weights[:, 2, :]
        piece = acc_sb[:, :, :].rearrange("p t f -> p (t f)")

        t_ps = ctx.enter_context(nc.psum_tensor("t_ps", [P, RING, 512], F32))
        acc = ctx.enter_context(nc.psum_tensor("acc", [P, TILES, 512], F32))
        mask_t = t_ps[:, :, :].bitcast(BF16)

        wa_loaded = sem("wa_loaded")
        ident_step = sem("ident_step")
        ident_ready = sem("ident_ready")
        w_turned = sem("w_turned")
        x_loaded = [sem(f"x_loaded{i}") for i in range(2)]
        x_turned = sem("x_turned")
        xt_hi_ready = sem("xt_hi_ready")
        xt_lo_ready = sem("xt_lo_ready")
        h_ready = sem("h_ready")
        h_hi_ready = sem("h_hi_ready")
        h_lo_ready = sem("h_lo_ready")
        sd_ready = sem("sd_ready")
        constants_ready = sem("constants_ready")
        w_parts_ready = sem("w_parts_ready")
        x_summed = sem("x_summed")
        x_sum_turned = sem("x_sum_turned")
        x_sum_ready = sem("x_sum_ready")
        setup_step = sem("setup_step")
        general_step = sem("general_step")
        piece_step = sem("piece_step")
        exponent_step = sem("exponent_step")
        norm_step = sem("norm_step")
        norm_end_step = sem("norm_end_step")
        waited = sem("waited")
        top_ready = sem("top_ready")
        top_all_ready = sem("top_all_ready")
        flag_ready = sem("flag_ready")
        ab_ready = sem("ab_ready")
        db_ready = sem("db_ready")
        ab_turned = sem("ab_turned")
        first_rows_turned = sem("first_rows_turned")
        first_rows_ready = sem("first_rows_ready")
        abt_ready = sem("abt_ready")
        rows_written = sem("rows_written")
        hsum_done = sem("hsum_done")
        hsum_ready = sem("hsum_ready")
        dst_written = sem("dst_written")
        piece_loaded = sem("piece_loaded")
        piece_used = sem("piece_used")
        exponent_ready = sem("exponent_ready")
        adj_loaded = [sem(f"adj_loaded{i}") for i in range(SLOTS)]
        rows_loaded = sem("rows_loaded")
        mask_ready = sem("mask_ready")
        bare_ready = sem("bare_ready")
        weights_ready = sem("weights_ready")
        hi_ready = sem("hi_ready")
        lo_vec = sem("lo_vec")
        lo_pool = sem("lo_pool")
        pair_done = sem("pair_done")
        acc_done = sem("acc_done")
        acc_free = sem("acc_free")
        acc_used = sem("acc_used")
        xres_loaded = sem("xres_loaded")
        var_ready = sem("var_ready")
        std_ready = sem("std_ready")
        out_ready = sem("out_ready")
        out_written = sem("out_written")

        def low_part_count(k):
            made, s = (POOL_LO, lo_pool) if k % BODY in POOL_LO else (VEC_LO, lo_vec)
            return s, len(made), made.index(k % BODY) + 1 + len(made) * (k // BODY)

        def wait_low_part(eng, turn, k):
            s, per_turn, rank = low_part_count(k)
            eng.wait_ge(s, turn * per_turn + (LO_CREDIT + rank))

        def chain(eng, step, start):
            made = [0]

            def link(instruction):
                made[0] += 1
                instruction.then_inc(step, 1)
                eng.wait_ge(step, start + made[0])
            return link

        block = ctx.enter_context(nc.Block())

        @block.sync
        def _(sp):
            sp.dma_start(w_in, W.rearrange("(o p) k -> p o k", p=P)).then_inc(wa_loaded, 16)
            with nc.allow_non_contiguous_dma(reason="256 words each"):
                sp.dma_start(a12[:, :, 0], a1.rearrange("(o p) -> p o", p=P)).then_inc(wa_loaded, 16)
                sp.dma_start(a12[:, :, 1], a2.rearrange("(o p) -> p o", p=P)).then_inc(wa_loaded, 16)
            for g in range(2):
                sp.dma_start(weights[:, g, :].rearrange("p (t f) -> p t f", t=TILES),
                             x_v[g]).then_inc(x_loaded[g], 16)
            with sp.Fori(0, CHUNKS // 2 - 1) as u:
                for g in range(2):
                    sp.wait_ge(x_summed, u * 2 + (g + 2))
                    sp.dma_start(weights[:, g, :].rearrange("p (t f) -> p t f", t=TILES),
                                 x_v[u * 2 + (g + 2)]).then_inc(x_loaded[g], 16)
            sp.wait_ge(abt_ready, 1)
            sp.dma_start(rows_dram.rearrange("a (t p) -> (a t) p", p=P), ab_t).then_inc(rows_written, 16)
            sp.wait_ge(rows_written, 16)

            def load_rows(chunk):
                for a in range(2):
                    src = rows_dram[a:a + 1, bass.ds(chunk * ROWS, ROWS)]
                    sp.dma_start(rows[:, a, :], src.to_broadcast([P, ROWS])).then_inc(rows_loaded, 16)

            sp.wait_ge(x_turned, CHUNKS)
            sp.dma_start(xres[:, :, :], x_v[0]).then_inc(xres_loaded, 16)

            with sp.Fori(0, CHUNKS - 1) as c:
                sp.wait_ge(bare_ready, c * PAIRS + PAIRS)
                load_rows(c + 1)
                sp.wait_ge(out_ready, c + 1)
                sp.dma_start(out_v[c], xres[:, :, :]).then_inc(out_written, 16)
                sp.wait_ge(out_written, c * 16 + 16)
                sp.dma_start(xres[:, :, :], x_v[c + 1]).then_inc(xres_loaded, 16)
            sp.wait_ge(bare_ready, TOTAL * BODY)
            load_rows(0)
            for half in range(2):
                part = slice(half * HALF, (half + 1) * HALF)
                sp.wait_ge(out_ready, CHUNKS + half)
                sp.dma_start(out_v[CHUNKS - 1][:, part, :], xres[:, part, :]).then_inc(out_written, 16)
            sp.wait_ge(out_written, (CHUNKS + 1) * 16)

        @block.gpsimd
        def _(pool):
            nc.gpsimd.memset(ident_bf[:, :], 0.0).then_inc(ident_step, 1)
            nc.gpsimd.memset(ident_f, 0.0).then_inc(ident_step, 1)
            pool.wait_ge(ident_step, 2)
            for m in (ident_bf[:, :], ident_f):
                nc.gpsimd.affine_select(out=m, in_=m, compare_op=ALU.not_equal, fill=1.0, base=0,
                                        pattern=[[-1, P]], channel_multiplier=1).then_inc(ident_ready, 1)
            nc.gpsimd.memset(x_sum, 0.0).then_inc(x_summed, 1)

            for s in range(SLOTS):
                pool.dma_start(adj_sb[:, s, :, :], adj_v[0, s]).then_inc(adj_loaded[s], 16)
            with pool.Fori(0, CHUNKS // 2) as u:
                for g in range(2):
                    pool.wait_ge(x_turned, u * 2 + (g + 1))
                    pool.wait_ge(x_summed, u * 2 + (g + 1))
                    nc.gpsimd.tensor_tensor(x_sum, x_sum, weights[:, g, :], ALU.add).then_inc(x_summed, 1)
            pool.wait_ge(top_ready, 1)
            nc.gpsimd.partition_all_reduce(top_all[:, :], top[:, :], P,
                                           bass.bass_isa.ReduceOp.max).then_inc(top_all_ready, 1)
            pool.sem_inc(lo_pool, LO_CREDIT)

            def turn(t, refill):
                for k in range(BODY):
                    if k in POOL_LO:
                        pool.wait_ge(hi_ready, t * BODY + (CREDIT + k + 1))
                        pool.wait_ge(pair_done, t * BODY + (CREDIT + k + 1 - RING))
                        nc.gpsimd.tensor_tensor(w_lo[:, k % RING, :], weights[:, k % RING, :],
                                                w_hi[:, k % RING, :].bitcast(F32),
                                                ALU.subtract).then_inc(lo_pool, 1)
                    if refill and k % 2 == 1:
                        pool.wait_ge(mask_ready, t * BODY + (k + 1))
                        nxt = t + 1
                        pool.dma_start(adj_sb[:, k // 2, :, :],
                                       adj_v[nxt // BODIES, (nxt % BODIES) * SLOTS + k // 2]
                                       ).then_inc(adj_loaded[k // 2], 16)

            with pool.Fori(0, TOTAL - 1) as t:
                turn(t, True)
            turn(TOTAL - 1, False)

        def act_split_x(act, g, n):
            act.wait_ge(x_turned, g + 1)
            for half in range(2):
                last = nc.scalar.copy(w_hi[:, n, half * 512:(half + 1) * 512], t_ps[:, 2 * (n % 2) + half, :])
            last.then_inc(xt_hi_ready, 1)

        def act_split_h(act, g):
            for t in range(TILES):
                act.wait_ge(h_ready, g * TILES + (t + 1))
                nc.scalar.copy(h_hi[:, g * TILES + t, 0:F], acc[:, t, 0:F]).then_inc(h_hi_ready, 1)

        def act_main(act, general):
            act.sem_inc(hi_ready, CREDIT)
            if not general:
                nc.scalar.preload_act_table(ACT.Sqrt)

            def exponential(s, count):
                act.wait_ge(exponent_ready, count)
                nc.scalar.activation(weights[:, s, :], weights[:, s, :], ACT.Exp).then_inc(bare_ready, 1)

            def high_part(t, k):
                act.wait_ge(weights_ready, t * BODY + (CREDIT + k + 1))
                act.wait_ge(pair_done, t * BODY + (CREDIT + k + 1 - RING))
                nc.scalar.copy(w_hi[:, k % RING, :], weights[:, k % RING, :]).then_inc(hi_ready, 1)
                if general:
                    exponential((k + 1) % RING, t * BODY + (k + 2))

            def evict(c, t):
                if t < TILES - 1:
                    act.wait_ge(acc_done, c * (TILES - 1) + (t + 1))
                else:
                    act.wait_ge(pair_done, c * PAIRS + (PAIRS + CREDIT))
                nc.scalar.copy(acc_sb[:, t, :], acc[:, t, 0:FA]).then_inc(acc_free, 1)

            def deviation(n, first=0, tiles=TILES):
                act.wait_ge(var_ready, n + 1)
                part = slice(first, first + tiles)
                nc.scalar.activation(row_stat[:, 3, part], row_stat[:, 2, part], ACT.Sqrt).then_inc(std_ready, 1)

            def first_turn(c, epilogue):
                for k in range(BODY):
                    high_part(c * BODIES, k)
                    if epilogue and k == 2:
                        act.wait_ge(acc_used, c)
                        for t in range(TILES):
                            evict(c - 1, t)
                    if epilogue and k == 5:
                        deviation(c - 1)

            def other_turns(c):
                with act.Fori(1, BODIES) as b:
                    for k in range(BODY):
                        high_part(c * BODIES + b, k)

            if general:
                exponential(0, 1)
            first_turn(0, False)
            other_turns(0)
            with act.Fori(1, CHUNKS) as c:
                first_turn(c, True)
                other_turns(c)
            act.wait_ge(acc_used, CHUNKS)
            for t in range(TILES):
                evict(CHUNKS - 1, t)
            for half in range(2):
                deviation(CHUNKS - 1 + half, half * HALF, HALF)

        @block.scalar
        def _(act):
            act.sem_inc(acc_free, TILES)
            nc.scalar.preload_act_table(ACT.Exp)
            act_split_x(act, 0, 0)
            with act.Fori(0, CHUNKS // 4 - 1) as u:
                for n in range(4):
                    act_split_x(act, u * 4 + (n + 1), (n + 1) % 4)
                    act_split_h(act, u * 4 + n)
            for n in range(CHUNKS - 4, CHUNKS - 1):
                act_split_x(act, n + 1, (n + 1) % 4)
                act_split_h(act, n)
            act.wait_ge(sd_ready, BLOCKS)
            act_split_h(act, CHUNKS - 1)
            act.wait_ge(flag_ready, 1)
            flag = act.value_load(unsafe[0:1, 0:1], min_val=0, max_val=1)
            with act.If(flag < 1):
                nc.scalar.activation(ab[:, 0:BLOCKS], src_dst[:, 0, :], ACT.Exp, bias=shift[:, 2:3],
                                     scale=SLOPE - 1.0).then_inc(ab_ready, 1)
                nc.scalar.activation(d_b[:, 1, :], src_dst[:, 1, :], ACT.Exp, bias=shift[:, 0:1], scale=1.0)
                nc.scalar.activation(d_b[:, 0, :], src_dst[:, 1, :], ACT.Exp, bias=shift[:, 1:2],
                                     scale=SLOPE).then_inc(db_ready, 1)
            with act.Else():
                act.wait_ge(hsum_ready, 1)
                with nc.allow_non_contiguous_dma(reason="a table of 8192 words, once"):
                    act.dma_start(dst_dram.rearrange("(t p) -> p t", p=P),
                                  src_dst[:, 1, :]).then_inc(dst_written, 16)
                act.wait_ge(dst_written, 16)
                with act.Fori(0, BLOCKS) as t:
                    with act.Fori(0, PIECES) as q:
                        act.wait_ge(piece_used, t * PIECES + (q + 1))
                        act.dma_start(piece[:, 0:PIECE].bitcast(I32), adj_rows_v[t, q]).then_inc(piece_loaded, 16)
                        act.dma_start(piece[:, PIECE:2 * PIECE],
                                      dst_dram.rearrange("(a n) -> a n", a=1)[:, bass.ds(q * PIECE, PIECE)]
                                      .to_broadcast([P, PIECE])).then_inc(piece_loaded, 16)
            for a in range(2):
                act.wait_ge(first_rows_turned, a + 1)
                nc.scalar.copy(rows[:, a, :], t_ps[:, 1 + a, :]).then_inc(first_rows_ready, 1)
            act.wait_ge(ab_turned, 1)
            nc.scalar.copy(ab_t, t_ps[:, 0, 0:P]).then_inc(abt_ready, 1)
            with act.If(flag < 1):
                act_main(act, False)
            with act.Else():
                act_main(act, True)

        def vec_main(dve, general):
            dve.sem_inc(weights_ready, CREDIT)
            dve.sem_inc(lo_vec, LO_CREDIT)
            dve.sem_inc(acc_used, 1)

            def bare(c, t, k, col):
                s = k % RING
                dve.wait_ge(hi_ready, t * BODY + (CREDIT + k + 1 - RING))
                wait_low_part(dve, t, k - RING)
                link = chain(dve, exponent_step, (t * BODY + k) * 4)
                for j in range(2):
                    w = weights[:, s, j * ROWS:(j + 1) * ROWS]
                    if not general:
                        last = nc.vector.tensor_scalar(w, rows[:, 0, :], d_b[:, 0, bass.ds(col + j, 1)],
                                                       d_b[:, 1, bass.ds(col + j, 1)], ALU.mult, ALU.max)
                        continue
                    link(nc.vector.tensor_scalar(w, rows[:, 1, :], d_b[:, 0, bass.ds(col + j, 1)], None, ALU.add))
                    link(nc.vector.scalar_tensor_tensor(w, rows[:, 0, :], src_dst[:, 1, bass.ds(col + j, 1)], w,
                                                        ALU.add, ALU.max))
                    last = nc.vector.tensor_scalar(w, w, HIGHEST_EXPONENT, None, ALU.min)
                last.then_inc(exponent_ready if general else bare_ready, 1)

            def masked(t, k):
                dve.wait_ge(bare_ready, t * BODY + (k + 1))
                dve.wait_ge(mask_ready, t * BODY + (k + 1))
                nc.vector.scalar_tensor_tensor(weights[:, k % RING, :], mask_t[:, k % RING, :], 0.0,
                                               weights[:, k % RING, :], ALU.not_equal,
                                               ALU.mult).then_inc(weights_ready, 1)

            def low_part(t, k):
                dve.wait_ge(hi_ready, t * BODY + (CREDIT + k + 1))
                dve.wait_ge(pair_done, t * BODY + (CREDIT + k + 1 - RING))
                nc.vector.tensor_tensor(w_lo[:, k % RING, :], weights[:, k % RING, :],
                                        w_hi[:, k % RING, :].bitcast(F32), ALU.subtract).then_inc(lo_vec, 1)

            def step(c, t, b, k):
                masked(t, k)
                if k >= 1 and (k - 1) in VEC_LO:
                    low_part(t, k - 1)
                if k + 1 < BODY:
                    bare(c, t, k + 1, b * (2 * BODY) + 2 * (k + 1))

            def start_next(c, t, b):
                bare(c, t + 1, 0, (b + 1) * (2 * BODY))

            def norm_sums(c, n, first=0, tiles=TILES):
                part = slice(first, first + tiles)
                each = range(first, first + tiles)
                dve.wait_ge(acc_free, c * TILES + (TILES + first + tiles))
                dve.wait_ge(xres_loaded, c * 16 + 16)
                link = chain(dve, norm_step, n * 6)
                den = acc_sb[:, part, F]
                link(nc.vector.tensor_scalar(row_stat[:, 0, part], den, 0.0, None, ALU.is_equal))
                link(nc.vector.scalar_tensor_tensor(row_stat[:, 1, part], row_stat[:, 0, part], float(N), den,
                                                    ALU.mult, ALU.add))
                link(nc.vector.reciprocal(row_stat[:, 1, part], row_stat[:, 1, part]))
                for t in each:
                    last = nc.vector.scalar_tensor_tensor(acc_sb[:, t, 0:F], hsum[:, :], row_stat[:, 0, t:t + 1],
                                                          acc_sb[:, t, 0:F], ALU.mult, ALU.add)
                link(last)
                for t in each:
                    last = nc.vector.scalar_tensor_tensor(xres[:, t, :], acc_sb[:, t, 0:F], row_stat[:, 1, t:t + 1],
                                                          xres[:, t, :], ALU.mult, ALU.add)
                last.then_inc(acc_used, 1)
                dve.wait_ge(acc_used, n + 2)
                for t in each:
                    last = nc.vector.bn_stats(bn[:, t, :], xres[:, t, :])
                link(last)
                dve.sem_inc(waited, 1)
                for t in each:
                    last = nc.vector.bn_aggr(mean_var[:, t, :], bn[:, t, :])
                link(last)
                nc.vector.tensor_scalar(row_stat[:, 2, part], mean_var[:, part, 1], EPS, None,
                                        ALU.add).then_inc(var_ready, 1)

            def normalise(n, first=0, tiles=TILES):
                part = slice(first, first + tiles)
                dve.wait_ge(std_ready, n + 1)
                link = chain(dve, norm_end_step, n)
                link(nc.vector.reciprocal(row_stat[:, 3, part], row_stat[:, 3, part]))
                for t in range(first, first + tiles):
                    last = nc.vector.tensor_scalar(xres[:, t, :], xres[:, t, :], mean_var[:, t, 0:1],
                                                   row_stat[:, 3, t:t + 1], ALU.subtract, ALU.mult)
                last.then_inc(out_ready, 1)

            def first_turn(c, epilogue):
                for k in range(BODY):
                    step(c, c * BODIES, 0, k)
                    if epilogue and k == 4:
                        norm_sums(c - 1, c - 1)
                    if epilogue and k == 6:
                        normalise(c - 1)
                start_next(c, c * BODIES, 0)

            def other_turns(c):
                with dve.Fori(1, BODIES - 1) as b:
                    for k in range(BODY):
                        step(c, c * BODIES + b, b, k)
                    start_next(c, c * BODIES + b, b)
                b = BODIES - 1
                for k in range(BODY):
                    step(c, c * BODIES + b, b, k)
                dve.wait_ge(rows_loaded, c * 32 + 32)
                bare(c + 1, c * BODIES + BODIES, 0, 0)

            dve.wait_ge(first_rows_ready, 2 if general else 1)
            bare(0, 0, 0, 0)
            first_turn(0, False)
            other_turns(0)
            with dve.Fori(1, CHUNKS) as c:
                first_turn(c, True)
                other_turns(c)
            for half in range(2):
                norm_sums(CHUNKS - 1, CHUNKS - 1 + half, half * HALF, HALF)
            for half in range(2):
                normalise(CHUNKS - 1 + half, half * HALF, HALF)

        @block.vector
        def _(dve):
            link = chain(dve, setup_step, 0)
            dve.sem_inc(h_lo_ready, TILES)
            dve.sem_inc(xt_lo_ready, 1)
            nc.vector.memset(square[0], 1.0).then_inc(constants_ready, 1)
            dve.wait_ge(w_turned, 1)
            nc.vector.tensor_copy(w_t[:, :, 0:F], t_ps[:, 2, :].rearrange("p (k o) -> p k o", k=2))
            link(nc.vector.tensor_copy(w_t[:, :, F:FA], t_ps[:, 3, 0:4].rearrange("p (k a) -> p k a", k=2)))
            link(nc.vector.tensor_copy(w_t_hi, w_t))
            nc.vector.tensor_tensor(w_t_lo, w_t, w_t_hi.bitcast(F32), ALU.subtract).then_inc(w_parts_ready, 1)
            nc.vector.memset(h_hi[:, 0:BLOCKS - 4, F:F + 1].bitcast(F32), 1.0)
            nc.vector.memset(h_hi[:, 0:BLOCKS - 4, F + 1:FA].bitcast(F32), 0.0)

            def split_x(g, n):
                dve.wait_ge(xt_hi_ready, g + 1)
                for half in range(2):
                    at = slice(half * 512, (half + 1) * 512)
                    last = nc.vector.tensor_tensor(w_lo[:, n, at], t_ps[:, 2 * (n % 2) + half, :],
                                                   w_hi[:, n, at].bitcast(F32), ALU.subtract)
                last.then_inc(xt_lo_ready, 1)

            def split_h(g, dots=True):
                for t in range(TILES):
                    n = g * TILES + t
                    dve.wait_ge(h_hi_ready, n + 1)
                    if dots:
                        nc.vector.tensor_copy(src_dst[:, :, bass.ds(n, 1)],
                                              acc[:, t, F:FA].rearrange("p (a o) -> p a o", o=1)
                                              ).then_inc(sd_ready, 1)
                    nc.vector.tensor_tensor(h_lo[:, n, :], acc[:, t, 0:F], h_hi[:, n, 0:F].bitcast(F32),
                                            ALU.subtract).then_inc(h_lo_ready, 1)

            split_x(0, 0)
            with dve.Fori(0, CHUNKS // 4 - 1) as u:
                for n in range(4):
                    split_x(u * 4 + (n + 1), (n + 1) % 4)
                    split_h(u * 4 + n)
            for n in range(CHUNKS - 4, CHUNKS - 1):
                split_x(n + 1, (n + 1) % 4)
                split_h(n)
            dve.wait_ge(h_ready, BLOCKS)
            nc.vector.tensor_copy(src_dst[:, :, BLOCKS - TILES:BLOCKS],
                                  acc[:, :, F:FA].rearrange("p t a -> p a t")).then_inc(sd_ready, TILES)
            dve.wait_ge(sd_ready, BLOCKS)
            link(nc.vector.tensor_scalar(d_b[:, :, :], src_dst[:, :, :], -1.0, None, ALU.mult))
            nc.vector.reduce_max(top[:, 0:2], src_dst[:, :, :], AX.X)
            nc.vector.reduce_max(top[:, 2:4], d_b[:, :, :], AX.X).then_inc(top_ready, 1)
            dve.wait_ge(x_sum_turned, 1)
            nc.vector.tensor_copy(xres[:, 1:3, P:2 * P],
                                  t_ps[:, 2, 0:2 * P].rearrange("p (k n) -> p k n", k=2)).then_inc(x_sum_ready, 1)
            dve.wait_ge(top_all_ready, 1)
            for n, factor in enumerate((-1.0, -SLOPE, SLOPE - 1.0)):
                nc.vector.tensor_scalar(shift[:, n:n + 1], top_all[:, 1:2], factor, None, ALU.mult)
            link(nc.vector.reduce_max(shift[:, 3:4], top_all[:, :], AX.X))
            nc.vector.tensor_scalar(unsafe[:, :], shift[:, 3:4], SAFE, None, ALU.is_gt).then_inc(flag_ready, 1)
            split_h(CHUNKS - 1, dots=False)
            dve.wait_ge(hsum_done, 1)
            nc.vector.tensor_copy(hsum[:, :], t_ps[:, 3, 0:F]).then_inc(hsum_ready, 1)
            dve.wait_ge(flag_ready, 1)
            flag = dve.value_load(unsafe[0:1, 0:1], min_val=0, max_val=1)
            with dve.If(flag < 1):
                nc.vector.memset(ab[:, BLOCKS:2 * BLOCKS], 0.0).then_inc(ab_ready, 1)
            with dve.Else():
                link = chain(dve, general_step, 0)
                link(nc.vector.memset(ab[:, BLOCKS:2 * BLOCKS], LOWEST))
                dve.sem_inc(piece_used, 1)
                with dve.Fori(0, BLOCKS) as t:
                    with dve.Fori(0, PIECES) as q:
                        link = chain(dve, piece_step, (t * PIECES + q) * 3)
                        link(nc.vector.memset(t_ps[:, 1, :], LOWEST))
                        dve.wait_ge(piece_loaded, (t * PIECES + q) * 32 + 32)
                        dve.sem_inc(waited, 1)
                        link(nc.vector.copy_predicated(t_ps[:, 1, :], piece[:, 0:PIECE].bitcast(I32),
                                                       piece[:, PIECE:2 * PIECE]))
                        link(nc.vector.reduce_max(shift[:, 0:1], t_ps[:, 1, :], AX.X))
                        nc.vector.tensor_tensor(ab[:, bass.ds(t + BLOCKS, 1)], ab[:, bass.ds(t + BLOCKS, 1)],
                                                shift[:, 0:1], ALU.max).then_inc(piece_used, 1)
                dve.wait_ge(piece_used, BLOCKS * PIECES + 1)
                link = chain(dve, general_step, 1)
                m, a, s = ab[:, BLOCKS:2 * BLOCKS], ab[:, 0:BLOCKS], src_dst[:, 0, :]
                link(nc.vector.tensor_tensor(m, m, s, ALU.add))
                link(nc.vector.scalar_tensor_tensor(m, m, SLOPE, m, ALU.mult, ALU.max))
                link(nc.vector.tensor_tensor(a, s, m, ALU.subtract))
                link(nc.vector.scalar_tensor_tensor(m, s, SLOPE, m, ALU.mult, ALU.subtract))
                link(nc.vector.tensor_scalar(d_b[:, 0, :], src_dst[:, 1, :], SLOPE, None, ALU.mult))
                dve.sem_inc(ab_ready, 2)
            nc.vector.memset(h_hi[:, BLOCKS - 4:BLOCKS, F:F + 1].bitcast(F32), 1.0)
            nc.vector.memset(h_hi[:, BLOCKS - 4:BLOCKS, F + 1:FA].bitcast(F32), 0.0).then_inc(constants_ready, 1)
            with dve.If(flag < 1):
                dve.wait_ge(db_ready, 1)
                vec_main(dve, False)
            with dve.Else():
                vec_main(dve, True)

        @block.tensor
        def _(pe):
            pe.sem_inc(pair_done, CREDIT)
            pe.wait_ge(ident_ready, 2)
            pe.wait_ge(wa_loaded, 48)
            for k in range(2):
                for o in range(2):
                    nc.tensor.transpose(t_ps[:, 2, k * F + o * P:k * F + (o + 1) * P],
                                        w_in[:, o, k * P:(k + 1) * P], ident_f)
            for k in range(2):
                for o in range(2):
                    last = nc.tensor.matmul(t_ps[:, 3, 2 * k:2 * k + 2], w_in[:, o, k * P:(k + 1) * P],
                                            a12[:, o, :], start=(o == 0), stop=(o == 1))
            last.then_inc(w_turned, 1)

            def turn_x(u, n):
                pe.wait_ge(x_loaded[n % 2], (u * 2 + n // 2) * 16 + 16)
                pe.wait_ge(xt_lo_ready, u * 4 + n)
                for t in range(TILES):
                    for k in range(2):
                        m = (t % 2) * 2 + k
                        last = nc.tensor.transpose(t_ps[:, 2 * (n % 2) + t // 2, m * P:(m + 1) * P],
                                                   weights[:, n % 2, t * F + k * P:t * F + (k + 1) * P], ident_f)
                last.then_inc(x_turned, 1)

            def product(out, n, t):
                for k in range(2):
                    at = slice((t * 2 + k) * P, (t * 2 + k + 1) * P)
                    nc.tensor.matmul(out, w_hi[:, n, at], w_t_hi[:, k, :], start=(k == 0), stop=False)
                    nc.tensor.matmul(out, w_hi[:, n, at], w_t_lo[:, k, :], start=False, stop=False)
                    last = nc.tensor.matmul(out, w_lo[:, n, at], w_t_hi[:, k, :], start=False, stop=(k == 1))
                return last

            def make_h(g, n):
                pe.wait_ge(xt_lo_ready, g + 2)
                for t in range(TILES):
                    pe.wait_ge(h_lo_ready, g * TILES + (t + 1))
                    product(acc[:, t, 0:FA], n, t).then_inc(h_ready, 1)

            turn_x(0, 0)
            pe.wait_ge(w_parts_ready, 1)
            with pe.Fori(0, CHUNKS // 4 - 1) as u:
                for n in range(4):
                    turn_x(u, n + 1)
                    make_h(u * 4 + n, n)
            for n in range(4):
                if n < 3:
                    turn_x(CHUNKS // 4 - 1, n + 1)
                make_h(CHUNKS - 4 + n, n)
            pe.wait_ge(x_summed, CHUNKS + 1)
            pe.wait_ge(constants_ready, 1)
            for k in range(2):
                for t in range(TILES):
                    last = nc.tensor.matmul(t_ps[:, 2, k * P:(k + 1) * P],
                                            x_sum[:, t * F + k * P:t * F + (k + 1) * P], square[0],
                                            start=(t == 0), stop=(t == TILES - 1))
            last.then_inc(x_sum_turned, 1)
            pe.wait_ge(x_sum_ready, 1)
            for k in range(2):
                last = nc.tensor.matmul(t_ps[:, 3, 0:F], square[1 + k], w_t[:, k, 0:F], start=(k == 0), stop=(k == 1))
            last.then_inc(hsum_done, 1)
            pe.wait_ge(ab_ready, 2)
            for a in range(2):
                for t in range(TILES):
                    last = nc.tensor.matmul(t_ps[:, 1 + a, t * P:(t + 1) * P],
                                            ab[:, a * BLOCKS + t:a * BLOCKS + t + 1].to_broadcast([P, P]),
                                            ident_f, start=True, stop=True)
                last.then_inc(first_rows_turned, 1)
            nc.tensor.transpose(t_ps[:, 0, 0:P], ab, ident_f).then_inc(ab_turned, 1)
            pe.wait_ge(abt_ready, 1)
            pe.wait_ge(hsum_ready, 1)

            def turn_mask(t, k):
                slot = (k % BODY) // 2
                if k % 2 == 0:
                    pe.wait_ge(adj_loaded[slot], (t + k // BODY) * 16 + 16)
                for j in range(2):
                    col = ((k % 2) * 2 + j) * P
                    for i in range(TILES):
                        last = nc.tensor.transpose(mask_t[:, k % RING, j * ROWS + i * P:j * ROWS + (i + 1) * P],
                                                   adj_sb[:, slot, i, col:col + P], ident_bf[:, :])
                last.then_inc(mask_ready, 1)

            def products(b, k, i, begin=False, end=False):
                for j in range(2):
                    n = b * (2 * BODY) + (2 * k + j)
                    at = slice(j * ROWS + i * P, j * ROWS + (i + 1) * P)
                    nc.tensor.matmul(acc[:, i, 0:FA], w_hi[:, k % RING, at], h_hi[:, n, :],
                                     start=begin and j == 0, stop=False)
                    nc.tensor.matmul(acc[:, i, 0:F], w_hi[:, k % RING, at], h_lo[:, n, :],
                                     start=False, stop=False)
                    last = nc.tensor.matmul(acc[:, i, 0:FA], w_lo[:, k % RING, at], h_hi[:, n, :],
                                            start=False, stop=end and j == 1)
                return last

            def next_mask(t, k):
                pe.wait_ge(hi_ready, t * BODY + (CREDIT + k + 1))
                turn_mask(t, k + LEAD)

            def turn(c, t, b, first, final):
                for k in range(BODY):
                    next_mask(t, k)
                    wait_low_part(pe, t, k)
                    for i in range(TILES):
                        if first and k == 0:
                            pe.wait_ge(acc_free, c * TILES + (i + 1))
                        end = final and k == BODY - 1
                        last = products(b, k, i, first and k == 0, end)
                        if end and i < TILES - 1:
                            last.then_inc(acc_done, 1)
                    last.then_inc(pair_done, 1)

            def last_turn():
                t, b = TOTAL - 1, BODIES - 1
                for k in range(BODY):
                    if k + LEAD < BODY:
                        next_mask(t, k)
                    wait_low_part(pe, t, k)
                    if k < BODY - TAIL:
                        for i in range(TILES):
                            last = products(b, k, i)
                        last.then_inc(pair_done, 1)
                for i in range(TILES):
                    for k in range(BODY - TAIL, BODY):
                        last = products(b, k, i, end=(k == BODY - 1))
                    if i < TILES - 1:
                        last.then_inc(acc_done, 1)
                last.then_inc(pair_done, TAIL)

            for k in range(LEAD):
                turn_mask(0, k)
            pe.wait_ge(h_lo_ready, BLOCKS + TILES)
            pe.wait_ge(constants_ready, 2)

            def turns_but_last(c):
                turn(c, c * BODIES, 0, True, False)
                with pe.Fori(1, BODIES - 1) as b:
                    turn(c, c * BODIES + b, b, False, False)

            with pe.Fori(0, CHUNKS - 1) as c:
                turns_but_last(c)
                turn(c, c * BODIES + (BODIES - 1), BODIES - 1, False, True)
            turns_but_last(CHUNKS - 1)
            last_turn()


_OUTS = [((N, F), "float32")]
_INS = ["x", "adj", "L0_gnn_W", "L0_gnn_a1", "L0_gnn_a2"]


def kernel(**inputs):
    import numpy as _np
    import concourse.bacc as _bacc
    from concourse import mybir as _mybir
    from concourse.bass_utils import run_bass_kernel_spmd as _run

    nc = _bacc.Bacc("TRN2", target_bir_lowering=False, num_devices=1)
    arrays, args = {}, []
    for name in _INS:
        a = _np.ascontiguousarray(inputs[name])
        arrays[f"in_{name}_dram"] = a
        args.append(nc.dram_tensor(f"in_{name}_dram", a.shape, _mybir.dt.from_np(a.dtype),
                                   kind="ExternalInput").ap())
    shape, dtype = _OUTS[0]
    args.append(nc.dram_tensor("out_0_dram", shape, _mybir.dt.from_np(_np.dtype(dtype)),
                               kind="ExternalOutput").ap())
    gat_kernel(nc, *args)
    r = _run(nc, [arrays], core_ids=[0])
    return r.results[0]["out_0_dram"]
```
